# Optimizing a Trainium2 kernel written in Bass

```python
import numpy as np
import jax
import jax.numpy as jnp

def _softmax(x, axis=-1):
    return jax.nn.softmax(x, axis=axis)

def _gelu(x):
    return jax.nn.gelu(x, approximate=True)

def _silu(x):
    return jax.nn.silu(x)

def _sigmoid(x):
    return jax.nn.sigmoid(x)

def _layernorm(x, axis=-1, eps=1e-05):
    m = jnp.mean(x, axis=axis, keepdims=True)
    v = jnp.var(x, axis=axis, keepdims=True)
    return (x - m) / jnp.sqrt(v + eps)

def _scatter_add(tgt, idx, src, axis=0):
    return tgt.at[idx].add(src)

def _segment_sum(src, seg, n):
    return jax.ops.segment_sum(src, seg, n)
kernel_name = 'mk_prb_d1_jaxref_r4_5c1961'

def setup_inputs(seed: int=0):
    np.random.seed(seed)
    _w = jnp.asarray

    def _L0_attn_setup():
        import jax, jax.numpy as jnp
        import numpy as np
        EPS = 1e-06
        CHUNK = 64
        GATE_LOGIT_NORMALIZER = 16.0
        NUM_HEADS = 4

        def _rms(x, w):
            return x * jax.lax.rsqrt(jnp.mean(x * x, axis=-1, keepdims=True) + EPS) * w

        def _gla_chunk(q, k, v, glog, num_heads):
            B, T, Dk = q.shape
            Dv = v.shape[-1]
            dk, dv = (Dk // num_heads, Dv // num_heads)
            Nc = T // CHUNK

            def split(x, d):
                return x.reshape(B, T, num_heads, d).transpose(0, 2, 1, 3).reshape(B, num_heads, Nc, CHUNK, d)
            q, k, v, g = (split(q, dk), split(k, dk), split(v, dv), split(glog, dk))
            b = jnp.cumsum(g, axis=3)
            scale = dk ** (-0.5)
            qe = q * jnp.exp(b) * scale
            mask = jnp.tril(jnp.ones((CHUNK, CHUNK), dtype=bool))
            A = jnp.einsum('bhncd,bhnsd->bhncs', qe, k * jnp.exp(-b))
            A = jnp.where(mask, A, 0.0)
            o_intra = jnp.einsum('bhncs,bhnsd->bhncd', A, v)

            def step(S, xs):
                qe_c, k_c, v_c, b_c = xs
                blast = b_c[:, :, -1, :]
                o_inter = jnp.einsum('bhcd,bhde->bhce', qe_c, S)
                kd = k_c * jnp.exp(blast[:, :, None, :] - b_c)
                S_new = S * jnp.exp(blast)[..., None] + jnp.einsum('bhcd,bhce->bhde', kd, v_c)
                return (S_new, o_inter)
            S0 = jnp.zeros((B, num_heads, dk, dv), q.dtype)
            xs = tuple((jnp.moveaxis(t, 2, 0) for t in (qe, k, v, b)))
            _, o_inter = jax.lax.scan(step, S0, xs)
            o = o_intra + jnp.moveaxis(o_inter, 0, 2)
            return o.reshape(B, num_heads, T, dv).transpose(0, 2, 1, 3)
        key = jax.random.key(seed)
        ks = jax.random.split(key, 12)
        B, T, Hs = (4, 512, 256)
        Dk, Dv, I, R = (128, 256, 704, 16)
        p = lambda k, s: jax.random.normal(k, s, jnp.float32) * 0.02
        return {'hidden_states': jax.random.normal(ks[0], (B, T, Hs), jnp.float32), 'attn_norm_w': jnp.ones((Hs,), jnp.float32), 'Wq': p(ks[1], (Hs, Dk)), 'Wk': p(ks[2], (Hs, Dk)), 'Wv': p(ks[3], (Hs, Dv)), 'Wg': p(ks[4], (Hs, Dv)), 'Wgk1': p(ks[5], (Hs, R)), 'Wgk2': p(ks[6], (R, Dk)), 'bgk2': jnp.zeros((Dk,), jnp.float32), 'gnorm_w': jnp.ones((Dv // NUM_HEADS,), jnp.float32), 'Wo': p(ks[7], (Dv, Hs)), 'mlp_norm_w': jnp.ones((Hs,), jnp.float32), 'W_gate': p(ks[8], (Hs, I)), 'W_up': p(ks[9], (Hs, I)), 'W_down': p(ks[10], (I, Hs))}
    _L0_attn_in = _L0_attn_setup()

    def _L0_ffn_setup():
        import jax, jax.numpy as jnp
        import numpy as np
        EPS = 1e-06
        TOP_K = 2

        def rms_norm(x, scale, eps=EPS):
            xf = x.astype(jnp.float32)
            mean_sq = jnp.mean(xf * xf, axis=-1, keepdims=True)
            return (xf * (scale.astype(jnp.float32) * jax.lax.rsqrt(mean_sq + eps))).astype(x.dtype)
        key = jax.random.key(seed)
        k0, k1, k2, k3 = jax.random.split(key, 4)
        B, S, D, H, E = (2, 512, 256, 704, 8)
        x = jax.random.normal(k0, (B, S, D), dtype=jnp.float32)
        norm_scale = jnp.ones((D,), dtype=jnp.float32)
        w_router = jax.random.normal(k1, (E, D), dtype=jnp.float32) * 0.02
        w_up = jax.random.normal(k2, (E, 2 * H, D), dtype=jnp.float32) * 0.02
        w_down = jax.random.normal(k3, (E, D, H), dtype=jnp.float32) * 0.02
        return {'x': x, 'norm_scale': norm_scale, 'w_router': w_router, 'w_up': w_up, 'w_down': w_down}
    _L0_ffn_in = _L0_ffn_setup()
    _d = {'L0_attn_hidden_states': _L0_attn_in['hidden_states'], 'L0_attn_attn_norm_w': _L0_attn_in['attn_norm_w'], 'L0_attn_Wq': _L0_attn_in['Wq'], 'L0_attn_Wk': _L0_attn_in['Wk'], 'L0_attn_Wv': _L0_attn_in['Wv'], 'L0_attn_Wg': _L0_attn_in['Wg'], 'L0_attn_Wgk1': _L0_attn_in['Wgk1'], 'L0_attn_Wgk2': _L0_attn_in['Wgk2'], 'L0_attn_bgk2': _L0_attn_in['bgk2'], 'L0_attn_gnorm_w': _L0_attn_in['gnorm_w'], 'L0_attn_Wo': _L0_attn_in['Wo'], 'L0_attn_mlp_norm_w': _L0_attn_in['mlp_norm_w'], 'L0_attn_W_gate': _L0_attn_in['W_gate'], 'L0_attn_W_up': _L0_attn_in['W_up'], 'L0_attn_W_down': _L0_attn_in['W_down'], 'L0_ffn_norm_scale': _L0_ffn_in['norm_scale'], 'L0_ffn_w_router': _L0_ffn_in['w_router'], 'L0_ffn_w_up': _L0_ffn_in['w_up'], 'L0_ffn_w_down': _L0_ffn_in['w_down']}
    _x0 = _d['L0_attn_hidden_states']
    _d['L0_attn_hidden_states'] = jax.random.normal(jax.random.fold_in(jax.random.key(seed), 1), (4, 1024, 256), dtype=_x0.dtype)
    del _x0
    return _d

def reference(L0_attn_hidden_states, L0_attn_attn_norm_w, L0_attn_Wq, L0_attn_Wk, L0_attn_Wv, L0_attn_Wg, L0_attn_Wgk1, L0_attn_Wgk2, L0_attn_bgk2, L0_attn_gnorm_w, L0_attn_Wo, L0_attn_mlp_norm_w, L0_attn_W_gate, L0_attn_W_up, L0_attn_W_down, L0_ffn_norm_scale, L0_ffn_w_router, L0_ffn_w_up, L0_ffn_w_down):

    def _L0_attn_ref(hidden_states, attn_norm_w, Wq, Wk, Wv, Wg, Wgk1, Wgk2, bgk2, gnorm_w, Wo, mlp_norm_w, W_gate, W_up, W_down):
        import jax, jax.numpy as jnp
        import numpy as np
        EPS = 1e-06
        CHUNK = 64
        GATE_LOGIT_NORMALIZER = 16.0
        NUM_HEADS = 4

        def _rms(x, w):
            return x * jax.lax.rsqrt(jnp.mean(x * x, axis=-1, keepdims=True) + EPS) * w

        def _gla_chunk(q, k, v, glog, num_heads):
            B, T, Dk = q.shape
            Dv = v.shape[-1]
            dk, dv = (Dk // num_heads, Dv // num_heads)
            Nc = T // CHUNK

            def split(x, d):
                return x.reshape(B, T, num_heads, d).transpose(0, 2, 1, 3).reshape(B, num_heads, Nc, CHUNK, d)
            q, k, v, g = (split(q, dk), split(k, dk), split(v, dv), split(glog, dk))
            b = jnp.cumsum(g, axis=3)
            scale = dk ** (-0.5)
            qe = q * jnp.exp(b) * scale
            mask = jnp.tril(jnp.ones((CHUNK, CHUNK), dtype=bool))
            A = jnp.einsum('bhncd,bhnsd->bhncs', qe, k * jnp.exp(-b))
            A = jnp.where(mask, A, 0.0)
            o_intra = jnp.einsum('bhncs,bhnsd->bhncd', A, v)

            def step(S, xs):
                qe_c, k_c, v_c, b_c = xs
                blast = b_c[:, :, -1, :]
                o_inter = jnp.einsum('bhcd,bhde->bhce', qe_c, S)
                kd = k_c * jnp.exp(blast[:, :, None, :] - b_c)
                S_new = S * jnp.exp(blast)[..., None] + jnp.einsum('bhcd,bhce->bhde', kd, v_c)
                return (S_new, o_inter)
            S0 = jnp.zeros((B, num_heads, dk, dv), q.dtype)
            xs = tuple((jnp.moveaxis(t, 2, 0) for t in (qe, k, v, b)))
            _, o_inter = jax.lax.scan(step, S0, xs)
            o = o_intra + jnp.moveaxis(o_inter, 0, 2)
            return o.reshape(B, num_heads, T, dv).transpose(0, 2, 1, 3)
        x = hidden_states
        h = _rms(x, attn_norm_w)
        q, k, v = (h @ Wq, h @ Wk, h @ Wv)
        glog = jax.nn.log_sigmoid(h @ Wgk1 @ Wgk2 + bgk2) / GATE_LOGIT_NORMALIZER
        o = _gla_chunk(q, k, v, glog, NUM_HEADS)
        g_out = (h @ Wg).reshape(o.shape)
        o = _rms(o, gnorm_w) * (g_out * jax.nn.sigmoid(g_out))
        attn_out = o.reshape(x.shape[0], x.shape[1], -1) @ Wo
        x2 = attn_out + x
        n = _rms(x2, mlp_norm_w)
        mlp = jax.nn.silu(n @ W_gate) * (n @ W_up) @ W_down
        return x2 + mlp

    def _L0_ffn_ref(x, norm_scale, w_router, w_up, w_down):
        import jax, jax.numpy as jnp
        import numpy as np
        EPS = 1e-06
        TOP_K = 2

        def rms_norm(x, scale, eps=EPS):
            xf = x.astype(jnp.float32)
            mean_sq = jnp.mean(xf * xf, axis=-1, keepdims=True)
            return (xf * (scale.astype(jnp.float32) * jax.lax.rsqrt(mean_sq + eps))).astype(x.dtype)
        skip = x
        xn = rms_norm(x, norm_scale)
        scores = jnp.einsum('bsd,ed->bse', xn, w_router)
        _, ids = jax.lax.top_k(scores, TOP_K)
        probs = jax.nn.softmax(scores, axis=-1)
        c = jnp.take_along_axis(probs, ids, axis=-1)
        h = jnp.einsum('bsd,ehd->bseh', xn, w_up)
        val, gate = jnp.split(h, 2, axis=-1)
        h = val * jax.nn.silu(gate)
        y = jnp.einsum('bseh,edh->bsed', h, w_down)
        yk = jnp.take_along_axis(y, ids[..., None], axis=2)
        out = jnp.sum(yk * c[..., None], axis=2)
        return out + skip
    x = L0_attn_hidden_states
    xn = _layernorm(x, axis=-1)
    x = x + _L0_attn_ref(xn, L0_attn_attn_norm_w, L0_attn_Wq, L0_attn_Wk, L0_attn_Wv, L0_attn_Wg, L0_attn_Wgk1, L0_attn_Wgk2, L0_attn_bgk2, L0_attn_gnorm_w, L0_attn_Wo, L0_attn_mlp_norm_w, L0_attn_W_gate, L0_attn_W_up, L0_attn_W_down) + _L0_ffn_ref(xn, L0_ffn_norm_scale, L0_ffn_w_router, L0_ffn_w_up, L0_ffn_w_down)
    return x

_drawn_inputs = setup_inputs


def setup_inputs(seed=0):
    import zlib

    import numpy as np

    out = dict(_drawn_inputs(seed))
    spreads = {'L0_attn_attn_norm_w': (1.0, 0.6),
     'L0_attn_bgk2': (0.0, 0.8),
     'L0_attn_gnorm_w': (1.0, 0.6),
     'L0_attn_mlp_norm_w': (1.0, 0.6),
     'L0_ffn_norm_scale': (1.0, 0.6)}
    factors = {'L0_attn_Wq': 2.969,
     'L0_attn_Wk': 2.96,
     'L0_attn_Wv': 2.949,
     'L0_attn_Wg': 2.994,
     'L0_attn_Wgk1': 8.0,
     'L0_attn_Wgk2': 8.0,
     'L0_attn_Wo': 2.973,
     'L0_attn_W_gate': 5.582,
     'L0_attn_W_up': 5.529,
     'L0_attn_W_down': 5.536,
     'L0_ffn_w_router': 8.0,
     'L0_ffn_w_up': 8.0,
     'L0_ffn_w_down': 8.0}
    for name, (base, spread) in spreads.items():
        noise = np.random.default_rng([zlib.crc32(name.encode()), seed]).standard_normal(out[name].shape)
        drawn = base * np.exp(spread * noise) if base else spread * noise
        out[name] = jnp.asarray(drawn.astype(out[name].dtype))
    for name, factor in factors.items():
        out[name] = (out[name] * factor).astype(out[name].dtype)
    return out
```

```python
from contextlib import ExitStack

import concourse.bass as bass
from concourse import mybir

ALU = mybir.AluOpType
ACT = mybir.ActivationFunctionType
AX = mybir.AxisListType.X
RMAX = bass.bass_isa.ReduceOp.max
F32 = mybir.dt.float32
F32R = mybir.dt.float32r
F16 = mybir.dt.float16
I32 = mybir.dt.int32

P = 128
U = 4
XS = 1024.0
WS = 8192.0
TINY = 1e-12


class Tile:

    def __init__(self, h, q):
        self.h, self.q = h, q
        self.i = h * U + q

    def back(self, k):
        d = (self.q - k) // U
        return Tile(self.h + d if d else self.h, (self.q - k) % U)


def wait(eng, sem, value):
    if isinstance(value, int) and value <= 0:
        return
    eng.wait_ge(sem, value)


def rep(ap, axis, n):
    a = ap.unsqueeze(axis)
    shape = list(a.shape)
    shape[axis] = n
    return a.to_broadcast(shape)


def program(nc, x, wqk, wvg, wgk1t, wgk2, bgk2, gnw, anw, mnw, fnw, wr, wo, wup, wdn, out):
    NTOK, D = x.shape
    NT = NTOK // P
    KD = D // P
    E = wr.shape[2]
    NH, TOPK, CH = 4, 2, 64
    DK, DV = wqk.shape[2] // 2, wvg.shape[2] // 2
    dk, dv = DK // NH, DV // NH
    QSCALE = float(dk) ** -0.5
    GSCALE = 1.0 / 16.0
    BT = 1024 // P
    R = E + 1
    NUP = wup.shape[3]
    HID = NUP // 2
    KH = (HID + P - 1) // P
    HT = HID - (KH - 1) * P
    MT = (NTOK * TOPK + E * (P - 1)) // P
    TT = NT + MT
    NSLOT = MT * P
    SL = [(0, 256), (256, 256), (512, HID - 512)]
    UPH, UPL, DNH, DNL = 0, KD * NUP, 2 * KD * NUP, 2 * KD * NUP + KH * D
    RW = DNL + KH * D
    ROW2 = NTOK + P
    assert KD == 2 and KH == 6 and NT == U * E and P == NH * dk and P == 2 * CH

    rows = nc.dram_tensor("rows", (ROW2 + NTOK, D), F32, kind="Internal").ap()
    meta = nc.dram_tensor("meta", (NSLOT, 2), I32, kind="Internal").ap()

    with ExitStack() as ctx:
        def sb(name, shape, dt=F32):
            return ctx.enter_context(nc.sbuf_tensor(name, shape, dt))

        made = {}

        def sem(name):
            if name not in made:
                made[name] = ctx.enter_context(nc.semaphore(name))
            return made[name]

        bank = [ctx.enter_context(nc.psum_tensor(f"bank{n}", [P, 512], F32)) for n in range(8)]

        ident = sb("ident", [P, P])
        ones = sb("ones", [P, P])
        tri = sb("tri", [P, P])
        fnw_sb = sb("fnw_sb", [P, KD])
        mnw_sb = sb("mnw_sb", [P, KD])
        nabs = sb("nabs", [P, 2, KD])
        nneg = sb("nneg", [P, 2, KD])
        scores = sb("scores", [P, NT, E])
        ids = sb("ids", [P, TT, 2], I32)
        tab = sb("tab", [P, TT, 3])
        etab = sb("etab", [P, TT], I32)
        ext = sb("ext", [P, 3, R])
        pairs = sb("pairs", [P, NT, TOPK, 2], I32)
        slot_i = sb("slot_i", [P, NT, TOPK], I32)
        meta_sb = sb("meta_sb", [P, MT, 2], I32)
        oneh = sb("oneh", [P, MT, E])
        iota_r = sb("iota_r", [P, E])
        ids2 = sb("ids2", [P, TT], I32)
        ptok = sb("ptok", [P, U, TOPK, 2], I32)
        pslot = sb("pslot", [P, U, TOPK], I32)
        stage_u = sb("stage_u", [P, KD, NUP])
        stage_d = sb("stage_d", [P, KH, D])
        xg = sb("xg", [P, U, D])
        idslot = sb("idslot", [P, U, 2], I32)
        tabslot = sb("tabslot", [P, U, 3])
        ysc = sb("ysc", [P, MT])
        xT_h = sb("xT_h", [P, 2, KD, P], F16)
        xT_l = sb("xT_l", [P, 2, KD, P], F16)
        sg = sb("sg", [P, HID])
        hid = sb("hid", [P, HID])
        hT_h = sb("hT_h", [P, KH, P], F16)
        hT_l = sb("hT_l", [P, KH, P], F16)
        yo = sb("yo", [P, U, D])
        pm = sb("pm", [P, KD])
        pmn = sb("pmn", [P, KD])
        pr = sb("pr", [P, 2])
        am = sb("am", [P, 2])
        amg = sb("amg", [P, 2])
        ia = sb("ia", [P, 2])
        am2 = sb("am2", [P, 1])
        fu = sb("fu", [P, KD])
        fd = sb("fd", [P, 1])
        wall0 = (nc.sbuf_base + 31) // 32 * 32
        wall = nc.alloc_sbuf_tensor_at("wall", [P, R, RW], F16, offset=wall0)
        assert wall0 + R * RW * 2 <= nc.sbuf_usable_end

        place = [wall0 + RW * 2]

        def over(name, shape, dt=F32):
            n = 4
            for s in shape[1:]:
                n *= s
            t = nc.alloc_sbuf_tensor_at(name, shape, dt, offset=place[0])
            place[0] += (n + 31) // 32 * 32
            assert place[0] <= wall0 + R * RW * 2
            return t

        CQ, CK, CV, CR, CO = DK, 2 * DK, 3 * DK, 3 * DK + 2 * DV, 3 * DK + 2 * DV + E
        NC1 = CO + D
        w1r = over("w1r", [P, KD, NC1])
        w1h = over("w1h", [P, KD, NC1], F32R)
        w1l = over("w1l", [P, KD, NC1], F32R)
        gk1_sb = over("gk1_sb", [16, D])
        gk2_sb = over("gk2_sb", [16, DK])
        bgk = over("bgk", [P, 1])
        anw_sb = over("anw_sb", [P, KD])
        gnw_sb = over("gnw_sb", [P, 1])
        cmask = over("cmask", [P, P])
        hmask = over("hmask", [P, NH])
        smask = over("smask", [P, P])
        keep = over("keep", [P, NT + 1])
        xin = over("xin", [P, U, D])
        xn = over("xn", [P, U, D])
        xs = over("xs", [P, U, D])
        st = over("st", [P, 6])
        mv = over("mv", [P, 2, 2])
        sd = over("sd", [P, 2, 2])
        ve = over("ve", [P, 2])
        half = over("half", [P, NH])
        xr = over("xr", [P, 2, D])
        xh = over("xh", [P, 2, KD, P], F32R)
        xl = over("xl", [P, 2, KD, P], F32R)
        au = over("au", [P, P])
        mu = over("mu", [P, P])
        e1 = over("e1", [P, P])
        le = over("le", [P, P])
        gl = over("gl", [P, P])
        bs = over("bs", [P, P])
        eb = over("eb", [P, 2, P])
        enb = over("enb", [P, P])
        qe = over("qe", [P, 2, P])
        ke = over("ke", [P, 2, P])
        qbd = over("qbd", [P, 2, NH, P])
        v_sb = over("v_sb", [P, 2, DV])
        eg = over("eg", [P, DV])
        gs1 = over("gs1", [P, DV])
        gs = over("gs", [P, 2, DV])
        at = over("at", [P, NH, P])
        ken = over("ken", [P, 2, 2, P])
        tst = over("tst", [P, dv])
        fac = over("fac", [P, 1])
        sbd = over("sbd", [P, 2, NH, dv])
        sq = over("sq", [P, DV])
        ss = over("ss", [P, NH])
        rh = over("rh", [P, NH])
        rhp = over("rhp", [P, NH])
        sig = over("sig", [P, DV])
        s2e = over("s2e", [P, 2])
        og1 = over("og1", [P, DV])
        og = over("og", [P, 2, DV])
        oh_ = over("ogT_h", [P, 2, P], F32R)
        ol_ = over("ogT_l", [P, 2, P], F32R)
        x2 = over("x2", [P, 2, D])
        sq2 = over("sq2", [P, D])
        s2 = over("s2", [P, 2])
        r2 = over("r2", [P, 2])
        n_sb = over("n_sb", [P, 2, D])
        b_sb = over("b_sb", [P, 2, D])
        zrow = over("zrow", [P, D])
        padm = over("padm", [P, MT, 2], I32)
        key = over("key", [P, NT, E])
        eqm = over("eqm", [P, NT, E])
        oh1 = over("oh1", [P, NT, E])
        oh2 = over("oh2", [P, NT, E])
        ohs = over("ohs", [P, NT, E])
        sc2 = over("sc2", [P, NT, E])
        ex = over("ex", [P, NT, E])
        m1 = over("m1", [P, NT])
        m2 = over("m2", [P, NT])
        ix = over("ix", [P, NT])
        den = over("den", [P, NT])
        rden = over("rden", [P, NT])
        em2 = over("em2", [P, NT])
        tot = over("tot", [P, E, NT])
        inc = over("inc", [P, E, NT])
        zm = over("zm", [P, E, NT])
        pad = over("pad", [P, E])
        rem = over("rem", [P, E], I32)
        end = over("end", [P, E])
        start = over("start", [P, E])
        slf = over("slf", [P, NT, TOPK])
        iota_e = over("iota_e", [P, E])
        iota_e8 = over("iota_e8", [P, E])
        iota_j = over("iota_j", [P, MT])
        cmp = over("cmp", [P, MT, E])
        rj = over("rj", [P, MT])
        NCST = 14 + 4 + NH + 8

        def part(r, first, n, p=P):
            return wall[0:p, bass.ds(r, 1), first:first + n].rearrange("p o n -> p (o n)")

        def up_ap(e, lo, k):
            return part(e, (UPH, UPL)[lo] + k * NUP, NUP)

        def dn_ap(e, lo):
            return part(e, (DNH, DNL)[lo], KH * D)

        def run2(eng, step):
            for q in range(U):
                step(0, q, q, 1)
            with eng.Fori(1, E - 1) as h:
                for q in range(U):
                    step(h, q, U + q, h + 1)
            for q in range(U):
                step(E - 1, q, (E - 1) * U + q, E, False)
            for q in range(U):
                step(E, q, NT + q)
            last = (TT - 1) // U
            with eng.Fori(E + 1, last) as h:
                for q in range(U):
                    step(h, q, (E + 1) * U + q)
            for i in range(last * U, TT + 4):
                step(i // U, i % U, i)


        block = ctx.enter_context(nc.Block())

        wsem = sem("weights_loaded")

        def phase1_done(eng):
            eng.wait_ge(sem("wo_done"), NT)
            eng.wait_ge(sem("n_ready"), NT)
            eng.wait_ge(sem("og1_ready"), NT)
            eng.wait_ge(sem("base_ready"), NT)
            for s in range(2):
                eng.wait_ge(sem(f"row_out{s}"), 16 * NT // 2)
                eng.wait_ge(sem(f"n_out{s}"), 16 * NT // 2)
                eng.wait_ge(sem(f"base_out{s}"), 16 * NT // 2)

        @block.sync
        def _(sp):
            for dst, src in (
                (w1r[:, :, CQ:CV], wqk.rearrange("k p n -> p k n")),
                (w1r[:, :, CV:CR], wvg.rearrange("k p n -> p k n")),
                (w1r[:, :, CR:CO], wr.rearrange("k p n -> p k n")),
                (w1r[:, :, CO:NC1], wo.rearrange("k p n -> p k n")),
                (gk1_sb[:], wgk1t), (gk2_sb[:], wgk2), (bgk[:], bgk2),
                (anw_sb[:], anw), (fnw_sb[:], fnw), (mnw_sb[:], mnw),
                (gnw_sb[0:dv, :], gnw), (gnw_sb[dv:2 * dv, :], gnw),
            ):
                sp.dma_start(dst, src).then_inc(wsem, 16)
            sp.dma_start(stage_u[:], wup[0].rearrange("k p n -> p k n")).then_inc(sem("stage_u_in"), 16)
            sp.dma_start(stage_d[:, 0:KH - 1, :], wdn[0, 0:(KH - 1) * P, :].rearrange("(c p) n -> p c n", p=P)).then_inc(sem("stage_d_in"), 16)
            sp.dma_start(stage_d[0:HT, KH - 1, :], wdn[0, (KH - 1) * P:HID, :]).then_inc(sem("stage_d_in"), 16)
            sp.wait_ge(sem("fill_ready"), 1)
            sp.dma_start(rows[NTOK:NTOK + P, :], zrow[:]).then_inc(sem("fill_out"), 16)

            def load(t):
                wait(sp, sem("xs_ready"), t.i - U + 1)
                wait(sp, sem("xr_ready"), t.i - U + 1)
                sp.dma_start(xin[:, t.q, :], x[bass.ds(t.i * P, P), :]).then_inc(sem(f"x_in{t.q}"), 16)

            def body(h, q, i):
                l = Tile(h, q)
                if i + 2 < NT:
                    load(l.back(-2))
                if i < NT:
                    sp.wait_ge(sem("xr_ready"), l.i + 1)
                    sp.dma_start(rows[bass.ds(l.i * P, P), :], xr[:, q % 2, :]).then_inc(sem(f"row_out{q % 2}"), 16)
                c = l.back(3)
                if 0 <= i - 3 < NT:
                    sp.wait_ge(sem("n_ready"), c.i + 1)
                    sp.dma_start(rows[bass.ds(c.i * P + ROW2, P), :], n_sb[:, c.q % 2, :]).then_inc(sem(f"n_out{c.q % 2}"), 16)
                    sp.wait_ge(sem("base_ready"), c.i + 1)
                    sp.dma_start(out[bass.ds(c.i * P, P), :], b_sb[:, c.q % 2, :]).then_inc(sem(f"base_out{c.q % 2}"), 16)

            def weights(e):
                sp.wait_ge(sem("up_lo"), 2 * e)
                sp.dma_start(stage_u[:], wup[bass.ds(e, 1), :, :, :].rearrange("o k p n -> p (o k) n")).then_inc(sem("stage_u_in"), 16)
                sp.wait_ge(sem("dn_lo"), e)
                sp.dma_start(stage_d[:, 0:KH - 1, :], wdn[bass.ds(e, 1), 0:(KH - 1) * P, :].rearrange("o (c p) n -> p (o c) n", p=P)).then_inc(sem("stage_d_in"), 16)
                sp.dma_start(stage_d[0:HT, KH - 1, :], wdn[bass.ds(e, 1), (KH - 1) * P:HID, :].rearrange("o p n -> (o p) n")).then_inc(sem("stage_d_in"), 16)

            load(Tile(0, 0))
            load(Tile(0, 1))
            for i in range(U):
                body(0, i, i)
            with sp.Fori(1, NT // U - 1) as h:
                for q in range(U):
                    body(h, q, U + q)
            weights(1)
            for i in range(NT - U, NT + 3):
                body(i // U, i % U, i)

            with sp.Fori(2, R) as e:
                weights(e)
            for q in range(U):
                sp.wait_ge(sem(f"meta_out{q}"), 16 * NT * TOPK // U)
            sp.dma_start(meta_sb[:], meta.rearrange("(j p) c -> p j c", p=P)).then_inc(sem("meta_in"), 16)

        @block.gpsimd
        def _(pool):
            g = nc.gpsimd
            g.memset(ident[:], 0.0).then_inc(sem("cst"), 1)
            g.memset(ones[:], 1.0).then_inc(sem("cst"), 1)
            g.memset(smask[:], 1.0).then_inc(sem("cst"), 1)
            g.memset(hmask[:], 0.0).then_inc(sem("cst"), 1)
            g.memset(keep[:], 1.0).then_inc(sem("cst"), 1)
            g.memset(ken[:], 0.0).then_inc(sem("cst"), 1)
            g.memset(tst[:], 0.0).then_inc(sem("cst"), 1)
            g.memset(fac[:], 0.0).then_inc(sem("cst"), 1)
            g.memset(zm[:], 1.0).then_inc(sem("cst"), 1)
            g.memset(half[:], -0.5).then_inc(sem("cst"), 1)
            g.memset(zrow[:], 0.0).then_inc(sem("fill_ready"), 1)
            g.iota(padm[:, :, 0], pattern=[[0, MT]], base=NTOK, channel_multiplier=1).then_inc(sem("padm"), 1)
            g.memset(padm[:, :, 1], 0).then_inc(sem("padm"), 1)
            pool.wait_ge(sem("padm"), 2)
            pool.wait_ge(sem("fill_ready"), 1)
            pool.wait_ge(sem("cst"), 10)
            g.dma_start(meta.rearrange("(j p) c -> p j c", p=P), padm[:]).then_inc(sem("added"), 16)
            g.memset(stage_d[HT:P, KH - 1, :], 0.0).then_inc(sem("cst"), 1)
            pool.wait_ge(sem("cst"), 11)
            g.affine_select(out=ident[:], in_=ident[:], compare_op=ALU.not_equal, fill=1.0, base=0,
                            pattern=[[-1, P]], channel_multiplier=1).then_inc(sem("cst"), 1)
            g.affine_select(out=tri[:], in_=ones[:], compare_op=ALU.is_gt, fill=0.0, base=0,
                            pattern=[[1, P]], channel_multiplier=-1).then_inc(sem("cst"), 1)
            g.affine_select(out=cmask[:], in_=ones[:], compare_op=ALU.is_ge, fill=0.0, base=0,
                            pattern=[[1, P]], channel_multiplier=-1).then_inc(sem("cst"), 1)
            pool.wait_ge(sem("cst"), 14)
            g.memset(cmask[0:CH, CH:P], 0.0).then_inc(sem("cst"), 1)
            pool.wait_ge(sem("cst"), 15)
            g.memset(smask[:, 0:P:CH], 0.0).then_inc(sem("cst"), 1)
            g.memset(keep[:, 0:NT + 1:BT], 0.0).then_inc(sem("cst"), 1)
            g.memset(zm[:, :, 0:1], 0.0).then_inc(sem("cst"), 1)
            for h in range(NH):
                pool.wait_ge(sem("cst"), 18 + h)
                g.memset(hmask[h * dk:(h + 1) * dk, h:h + 1], 1.0).then_inc(sem("cst"), 1)
            pool.wait_ge(sem("cst"), 18 + NH)
            g.iota(iota_e[:], pattern=[[1, E]], base=0, channel_multiplier=0, allow_small_or_imprecise_dtypes=True).then_inc(sem("cst"), 1)
            g.iota(iota_e8[:], pattern=[[1, E]], base=E, channel_multiplier=0, allow_small_or_imprecise_dtypes=True).then_inc(sem("cst"), 1)
            g.iota(iota_r[:], pattern=[[1, E]], base=1, channel_multiplier=0, allow_small_or_imprecise_dtypes=True).then_inc(sem("cst"), 1)
            g.iota(iota_j[:], pattern=[[P, MT]], base=0, channel_multiplier=0, allow_small_or_imprecise_dtypes=True).then_inc(sem("cst"), 1)
            g.iota(ids[:, 0:NT, 0], pattern=[[P, NT]], base=ROW2, channel_multiplier=1).then_inc(sem("cst"), 1)
            g.iota(ids[:, 0:NT, 1], pattern=[[P, NT]], base=0, channel_multiplier=1).then_inc(sem("cst"), 1)
            g.memset(etab[:, 0:NT], 0).then_inc(sem("cst"), 1)
            g.iota(pairs[:, :, :, 0], pattern=[[P, NT], [0, TOPK]], base=0, channel_multiplier=1).then_inc(sem("cst"), 1)

            def allreduce(col):
                g.partition_all_reduce(am[:, col:col + 1], pr[:, col:col + 1], P, RMAX).then_inc(sem("am_up" if col == 0 else "am_dn"), 1)


            def body(h, q, i):
                l = Tile(h, q)
                a, b, c = l.back(1), l.back(2), l.back(3)
                if i < NT:
                    pool.wait_ge(sem("ve_ready"), 2 * l.i + 2)
                    wait(pool, sem("xr_ready"), l.i - 1)
                    g.tensor_tensor(sd[:, q % 2, :], ve[:], half[:, 0:2], ALU.pow).then_inc(sem("sd_ready"), 1)
                if 0 <= i - 1 < NT:
                    pool.wait_ge(sem("qe_ready"), a.i + 1)
                    wait(pool, sem("a_done"), a.i - 1)
                    g.tensor_tensor(qbd[:, a.q % 2, :, :], rep(qe[:, a.q % 2, :], 1, NH), rep(hmask[:], 2, P), ALU.mult).then_inc(sem("qbd_ready"), 1)
                if 0 <= i - 3 < NT:
                    pool.wait_ge(sem("s2e_ready"), c.i + 1)
                    wait(pool, sem("n_ready"), c.i - 1)
                    g.tensor_tensor(r2[:, c.q % 2:c.q % 2 + 1], s2e[:, c.q % 2:c.q % 2 + 1], half[:, 0:1], ALU.pow).then_inc(sem("r2_ready"), 1)
                if 0 <= i - 2 < NT:
                    pool.wait_ge(sem("rh_ready"), b.i + 1)
                    wait(pool, sem("og1_ready"), b.i)
                    g.tensor_tensor(rhp[:], rh[:], half[:], ALU.pow).then_inc(sem("rhp_ready"), 1)
                if i < NT:
                    pool.wait_ge(sem("xn_ready"), l.i + 1)
                    wait(pool, sem("base_ready"), l.i - U + 1)
                    g.tensor_tensor(xs[:, q, :], xin[:, q, :], xn[:, q, :], ALU.add).then_inc(sem("xs_ready"), 1)
                if 0 <= i - 2 < NT:
                    pool.wait_ge(sem("og1_ready"), b.i + 1)
                    wait(pool, sem("t2_done"), b.i - 1)
                    g.tensor_tensor(og[:, b.q % 2, :], og1[:], gs[:, b.q % 2, :], ALU.mult).then_inc(sem("og_ready"), 1)
                if 0 <= i - 3 < NT:
                    pool.wait_ge(sem("x2_ready"), c.i + 1)
                    wait(pool, sem(f"base_out{(c.q + 1) % 2}"), 8 * (c.i - 1 - (c.q + 1) % 2) + 16)
                    g.tensor_tensor(b_sb[:, c.q % 2, :], x2[:, c.q % 2, :], xs[:, c.q, :], ALU.add).then_inc(sem("base_ready"), 1)

            for i in range(U):
                body(0, i, i)
                if i == 1:
                    pool.wait_ge(sem("pr_up"), 1)
                    allreduce(0)
                    pool.wait_ge(sem("pr_dn"), 1)
                    allreduce(1)
            with pool.Fori(1, NT // U) as h:
                for q in range(U):
                    body(h, q, U + q)
            for i in range(NT, NT + 3):
                body(i // U, i % U, i)

            phase1_done(pool)
            pool.wait_ge(sem("fill_out"), 16)
            pool.wait_ge(sem("added"), 16)
            pool.wait_ge(sem("slots_ready"), 2)

            def step(h, q, i, e=None, more=True):
                t = Tile(h, q)
                w = t.back(4)
                if i == NT:
                    pool.wait_ge(sem("tab_full"), 4)
                add = i >= 4 and i - 4 < TT
                if add:
                    pool.wait_ge(sem("y_ready"), w.i + 1)
                    wait(pool, sem("added"), w.i * 16 + 16)
                    g.tensor_copy(idslot[:, q, 1:2], ids2[:, bass.ds(w.i, 1)]).then_inc(sem("sid_ready"), 1)
                if i < TT:
                    wait(pool, sem("xt_done"), t.i - 3)
                    g.tensor_copy(idslot[:, q, 0:1], ids[:, bass.ds(t.i, 1), 0]).then_inc(sem("id_ready"), 1)
                if i < NT:
                    wait(pool, sem(f"meta_out{q}"), h * 16 * TOPK)
                    for k in range(TOPK):
                        g.tensor_copy(ptok[:, q, k, :], pairs[:, bass.ds(t.i, 1), k, :].rearrange("p o c -> p (o c)")).then_inc(sem("pt_ready"), 1)
                        g.tensor_copy(pslot[:, q, k:k + 1], slot_i[:, bass.ds(t.i, 1), k]).then_inc(sem("pt_ready"), 1)
                    pool.wait_ge(sem("pt_ready"), (t.i + 1) * 2 * TOPK)
                if add:
                    pool.wait_ge(sem("sid_ready"), w.i + 1)
                if e is not None and q < 2:
                    pool.wait_ge(sem("pr_up" if q == 0 else "pr_dn"), e + 1)
                if i < TT:
                    pool.wait_ge(sem("id_ready"), t.i + 1)
                    g.tensor_copy(tabslot[:, q, :], tab[:, bass.ds(t.i, 1), :].rearrange("p o c -> p (o c)")).then_inc(sem("tab_ready"), 1)
                    g.indirect_dma_start(out=xg[:, q, :], out_offset=None, in_=rows,
                                         in_offset=bass.IndirectOffsetOnAxis(ap=idslot[:, q, 0:1], axis=0)).then_inc(sem(f"x_gat{q}"), 16)
                if add:
                    g.indirect_dma_start(out=out, out_offset=bass.IndirectOffsetOnAxis(ap=idslot[:, q, 1:2], axis=0),
                                         in_=yo[:, q, :], in_offset=None, bounds_check=NTOK - 1, oob_is_err=False,
                                         compute_op=ALU.add).then_inc(sem("added"), 16)
                if i < NT:
                    for k in range(TOPK):
                        g.indirect_dma_start(out=meta, out_offset=bass.IndirectOffsetOnAxis(ap=pslot[:, q, k:k + 1], axis=0),
                                             in_=ptok[:, q, k, :], in_offset=None).then_inc(sem(f"meta_out{q}"), 16)
                if e is not None and q < 2:
                    allreduce(q)

            run2(pool, step)
            pool.wait_ge(sem("added"), 16 * TT + 16)

        @block.scalar
        def _(act):
            s = nc.scalar
            for k in range(KD):
                act.wait_ge(sem("w1_scaled"), k + 1)
                s.activation(w1h[:, k, :], w1r[:, k, :], ACT.Copy).then_inc(sem("w1_hi"), 1)

            def hi_up(e, k):
                act.wait_ge(sem("fu_ready"), e + 1)
                s.activation(up_ap(e, 0, k), stage_u[:, k, :], ACT.Copy, scale=fu[:, k:k + 1]).then_inc(sem("up_hi"), 1)

            def hi_dn(e):
                act.wait_ge(sem("fd_ready"), e + 1)
                s.activation(dn_ap(e, 0), stage_d[:].rearrange("p c n -> p (c n)"), ACT.Copy, scale=fd[:]).then_inc(sem("dn_hi"), 1)

            def body(h, q, i):
                l = Tile(h, q)
                a, b, c = l.back(1), l.back(2), l.back(3)
                A, B, C = 0 <= i - 1 < NT, 0 <= i - 2 < NT, 0 <= i - 3 < NT
                ap, bp, cp = a.q % 2, b.q % 2, c.q % 2
                if A:
                    act.wait_ge(sem("t1_done"), a.i + 1)
                    wait(act, sem("vg_done"), a.i - 1)
                    s.activation(xh[:, ap].rearrange("p k n -> p (k n)"), bank[0][:, 0:D], ACT.Copy).then_inc(sem("xh_ready"), 1)
                if B:
                    act.wait_ge(sem("kt_done"), b.i + 1)
                    wait(act, sem("m_done"), b.i - 1)
                    s.activation(ken[0:CH, bp, 0, :], bank[4][0:CH, P:2 * P], ACT.Copy).then_inc(sem("ken_ready"), 1)
                    s.activation(ken[CH:P, bp, 1, :], bank[4][CH:P, P:2 * P], ACT.Copy).then_inc(sem("ken_ready"), 1)
                if C:
                    act.wait_ge(sem("t2_done"), c.i + 1)
                    wait(act, sem("wo_done"), c.i)
                    s.activation(oh_[:].rearrange("p k n -> p (k n)"), bank[6][:, 0:D], ACT.Copy).then_inc(sem("oh_ready"), 1)
                if A:
                    act.wait_ge(sem("qk_done"), a.i + 1)
                    s.activation(au[:], bank[1][:, 0:P], ACT.Abs, bias=bgk[:]).then_inc(sem("au_ready"), 1)
                    act.wait_ge(sem("au_ready"), a.i + 1)
                    s.activation(e1[:], au[:], ACT.Exp, scale=-1.0).then_inc(sem("e1_ready"), 1)
                    act.wait_ge(sem("e1_ready"), a.i + 1)
                    wait(act, sem("gl_ready"), a.i)
                    s.activation(le[:], e1[:], ACT.Ln, bias=ones[:, 0:1]).then_inc(sem("le_ready"), 1)
                    act.wait_ge(sem("vg_done"), a.i + 1)
                    wait(act, sem("m_done"), a.i - 1)
                    wait(act, sem("o_done"), a.i - 1)
                    s.activation(v_sb[:, ap, :], bank[2][:, 0:DV], ACT.Copy).then_inc(sem("v_ready"), 1)
                    wait(act, sem("gs1_ready"), a.i)
                    s.activation(eg[:], bank[2][:, DV:2 * DV], ACT.Exp, scale=-1.0).then_inc(sem("eg_ready"), 1)
                if C:
                    act.wait_ge(sem("x2_ready"), c.i + 1)
                    s.activation(sq2[:], x2[:, cp, :], ACT.Square, accum_out=s2[:, cp:cp + 1]).then_inc(sem("s2_ready"), 1)
                if A:
                    act.wait_ge(sem("bs_ready"), a.i + 1)
                    wait(act, sem("st_steps"), 5 * (a.i - 1))
                    s.activation(eb[:, ap, :], bs[:], ACT.Exp, scale=GSCALE).then_inc(sem("eb_ready"), 1)
                    wait(act, sem("ke_ready"), a.i)
                    s.activation(enb[:], bs[:], ACT.Exp, scale=-GSCALE).then_inc(sem("enb_ready"), 1)
                if C:
                    act.wait_ge(sem("r2_ready"), c.i + 1)
                    wait(act, sem(f"n_out{1 - cp}"), 8 * (c.i - 1 - (1 - cp)) + 16)
                    s.activation(n_sb[:, cp, :], x2[:, cp, :], ACT.Copy, scale=r2[:, cp:cp + 1]).then_inc(sem("n_ready"), 1)
                if B:
                    act.wait_ge(sem("o_done"), b.i + 1)
                    wait(act, sem("ss_ready"), b.i)
                    s.activation(sq[:], bank[5][:, 0:DV], ACT.Square).then_inc(sem("sq_ready"), 1)

            for i in range(U):
                body(0, i, i)
                if i == 1:
                    hi_up(0, 0)
                    hi_up(0, 1)
                if i == 2:
                    hi_dn(0)
            with act.Fori(1, NT // U) as h:
                for q in range(U):
                    body(h, q, U + q)
            for i in range(NT, NT + 3):
                body(i // U, i % U, i)
            act.wait_ge(sem("rt_ex"), 1)
            s.activation(ex[:].rearrange("p t e -> p (t e)"), sc2[:].rearrange("p t e -> p (t e)"), ACT.Exp).then_inc(sem("ex_ready"), 1)
            act.wait_ge(sem("rt_em2"), 1)
            s.activation(em2[:], m2[:], ACT.Exp).then_inc(sem("ex_ready"), 1)
            phase1_done(act)

            def step(h, q, i, e=None, more=True):
                t = Tile(h, q)
                u, d = t.back(1), t.back(2)
                if 0 <= i - 2 < TT:
                    act.wait_ge(sem("ht_done"), d.i + 1)
                    wait(act, sem("dn_done"), d.i)
                    s.activation(hT_h[:, 0:4, :].rearrange("p c n -> p (c n)"), bank[5][:], ACT.Copy).then_inc(sem("hth_ready"), 1)
                    s.activation(hT_h[:, 4, :], bank[6][:, 0:P], ACT.Copy).then_inc(sem("hth_ready"), 1)
                    s.activation(hT_h[0:HT, 5, :], bank[6][0:HT, P:2 * P], ACT.Copy).then_inc(sem("hth_ready"), 1)
                if i < TT:
                    act.wait_ge(sem("xt_done"), t.i + 1)
                    wait(act, sem("up_done"), 3 * (t.i - 1))
                    s.activation(xT_h[:, q % 2].rearrange("p k n -> p (k n)"), bank[0][:, 0:D], ACT.Copy, scale=XS).then_inc(sem("xth_ready"), 1)
                if 0 <= i - 1 < TT:
                    act.wait_ge(sem("tab_ready"), u.i + 1)
                    for n, (o, w) in enumerate(SL):
                        act.wait_ge(sem("up_done"), 3 * u.i + n + 1)
                        wait(act, sem("h_ready"), 3 * (u.i - 1) + n + 1)
                        s.activation(sg[:, o:o + w], bank[1 + n][:, 0:w], ACT.Silu, scale=tabslot[:, u.q, 0:1]).then_inc(sem("sg_ready"), 1)
                if e is not None:
                    if q < 2:
                        hi_up(e, q)
                    if q == 2:
                        hi_dn(e)

            run2(act, step)

        @block.vector
        def _(dve):
            v = nc.vector
            dve.wait_ge(wsem, 16 * 12)
            dve.wait_ge(sem("gk_done"), 2)
            for k in range(KD):
                v.tensor_scalar(w1r[:, k, 0:DK], bank[0][:, k * DK:(k + 1) * DK], anw_sb[:, k:k + 1], None, ALU.mult).then_inc(sem("w1_steps"), 1)
                v.tensor_scalar(w1r[:, k, CQ:CR], w1r[:, k, CQ:CR], anw_sb[:, k:k + 1], None, ALU.mult).then_inc(sem("w1_steps"), 1)
                v.tensor_scalar(w1r[:, k, CR:CO], w1r[:, k, CR:CO], fnw_sb[:, k:k + 1], None, ALU.mult).then_inc(sem("w1_steps"), 1)
                v.tensor_scalar(w1r[:, k, CO:NC1], w1r[:, k, CO:NC1], gnw_sb[:], None, ALU.mult).then_inc(sem("w1_scaled"), 1)
            for n, w in enumerate((mnw_sb, fnw_sb)):
                v.tensor_scalar(nneg[:, n, :], w[:], -1.0, None, ALU.mult).then_inc(sem("nabs_ready"), 1)
                dve.wait_ge(sem("nabs_ready"), 2 * n + 1)
                v.tensor_tensor(nabs[:, n, :], nneg[:, n, :], w[:], ALU.max).then_inc(sem("nabs_ready"), 1)
            dve.wait_ge(sem("w1_steps"), 3 * KD)
            for k in range(KD):
                dve.wait_ge(sem("w1_hi"), k + 1)
                v.tensor_tensor(w1l[:, k, :], w1r[:, k, :], w1h[:, k, :].bitcast(F32), ALU.subtract).then_inc(sem("w1_lo"), 1)
            dve.wait_ge(sem("cst"), NCST)

            def amax_up(e, n):
                dve.wait_ge(sem("stage_u_in"), (e + 1) * 16)
                v.tensor_reduce(pm[:], stage_u[:], AX, ALU.max, apply_absolute_value=True).then_inc(sem("pm_steps"), 1)
                dve.wait_ge(sem("pm_steps"), 2 * e + 1)
                v.tensor_tensor(pmn[:], pm[:], nabs[:, n, :], ALU.mult).then_inc(sem("pm_steps"), 1)
                dve.wait_ge(sem("pm_steps"), 2 * e + 2)
                v.tensor_reduce(pr[:, 0:1], pmn[:], AX, ALU.max).then_inc(sem("pr_up"), 1)

            def amax_dn(e):
                dve.wait_ge(sem("stage_d_in"), (e + 1) * 32)
                v.tensor_reduce(pr[:, 1:2], stage_d[:].rearrange("p c n -> p (c n)"), AX, ALU.max, apply_absolute_value=True).then_inc(sem("pr_dn"), 1)

            def scale_up(e, nw):
                n = sem("su_steps")
                dve.wait_ge(sem("am_up"), e + 1)
                v.tensor_scalar(amg[:, 0:1], am[:, 0:1], TINY, None, ALU.max).then_inc(n, 1)
                dve.wait_ge(n, 3 * e + 1)
                v.reciprocal(ia[:, 0:1], amg[:, 0:1]).then_inc(n, 1)
                v.tensor_scalar(ext[:, 0, bass.ds(e, 1)], amg[:, 0:1], 1.0 / (WS * XS), None, ALU.mult).then_inc(n, 1)
                dve.wait_ge(n, 3 * e + 3)
                v.tensor_scalar(fu[:], nw[:], ia[:, 0:1], WS, ALU.mult, ALU.mult).then_inc(sem("fu_ready"), 1)
                v.tensor_scalar(ext[:, 1, bass.ds(e, 1)], ia[:, 0:1], 0.5 / (WS * XS), None, ALU.mult).then_inc(sem("kap_ready"), 1)

            def scale_dn(e):
                n = sem("sd_steps")
                dve.wait_ge(sem("am_dn"), e + 1)
                v.tensor_scalar(amg[:, 1:2], am[:, 1:2], TINY, None, ALU.max).then_inc(n, 1)
                dve.wait_ge(n, 4 * e + 1)
                v.reciprocal(ia[:, 1:2], amg[:, 1:2]).then_inc(n, 1)
                v.tensor_tensor(am2[:], amg[:, 0:1], amg[:, 0:1], ALU.mult).then_inc(n, 1)
                dve.wait_ge(n, 4 * e + 3)
                v.tensor_scalar(fd[:], ia[:, 1:2], WS, None, ALU.mult).then_inc(sem("fd_ready"), 1)
                v.tensor_scalar(ext[:, 2, bass.ds(e, 1)], am2[:], amg[:, 1:2], 2.0 / WS, ALU.mult, ALU.mult).then_inc(n, 1)

            def lo_up(e, k):
                dve.wait_ge(sem("up_hi"), 2 * e + k + 1)
                v.scalar_tensor_tensor(up_ap(e, 1, k), stage_u[:, k, :], fu[:, k:k + 1], up_ap(e, 0, k), ALU.mult, ALU.subtract).then_inc(sem("up_lo"), 1)

            def lo_dn(e):
                dve.wait_ge(sem("dn_hi"), e + 1)
                v.scalar_tensor_tensor(dn_ap(e, 1), stage_d[:].rearrange("p c n -> p (c n)"), fd[:], dn_ap(e, 0), ALU.mult, ALU.subtract).then_inc(sem("dn_lo"), 1)

            def low_rows(a):
                ap = a.q % 2
                dve.wait_ge(sem("xh_ready"), a.i + 1)
                v.tensor_tensor(xl[:, ap].rearrange("p k n -> p (k n)"), bank[0][:, 0:D],
                                xh[:, ap].rearrange("p k n -> p (k n)").bitcast(F32), ALU.subtract).then_inc(sem("xl_ready"), 1)

            def body(h, q, i):
                l = Tile(h, q)
                a, b, c = l.back(1), l.back(2), l.back(3)
                A, B, C = 0 <= i - 1 < NT, 0 <= i - 2 < NT, 0 <= i - 3 < NT
                ap, bp, cp = a.q % 2, b.q % 2, c.q % 2
                if i < NT:
                    n = sem("ln_steps")
                    dve.wait_ge(sem(f"x_in{q}"), 16 * h + 16)
                    v.bn_stats(st[:], xin[:, q, :]).then_inc(n, 1)
                    dve.wait_ge(n, 2 * l.i + 1)
                    if A:
                        low_rows(a)
                    v.bn_aggr(mv[:, q % 2, :], st[:]).then_inc(n, 1)
                    dve.wait_ge(n, 2 * l.i + 2)
                    wait(dve, sem("sd_ready"), l.i)
                    v.tensor_scalar(ve[:, 0:1], mv[:, q % 2, 1:2], 1e-5, None, ALU.add).then_inc(sem("ve_ready"), 1)
                    v.tensor_scalar(ve[:, 1:2], mv[:, q % 2, 1:2], 1.0 + 1e-6, 1e-11, ALU.mult, ALU.add).then_inc(sem("ve_ready"), 1)
                elif A:
                    low_rows(a)
                if B:
                    dve.wait_ge(sem("a_done"), b.i + 1)
                    wait(dve, sem("o_done"), b.i)
                    v.tensor_tensor(at[:], bank[3][:].rearrange("p (h n) -> p h n", h=NH), rep(cmask[:], 1, NH), ALU.mult).then_inc(sem("at_ready"), 1)
                if C:
                    dve.wait_ge(sem("oh_ready"), c.i + 1)
                    v.tensor_tensor(ol_[:].rearrange("p k n -> p (k n)"), bank[6][:, 0:D],
                                    oh_[:].rearrange("p k n -> p (k n)").bitcast(F32), ALU.subtract).then_inc(sem("ol_ready"), 1)
                if A:
                    dve.wait_ge(sem("qk_done"), a.i + 1)
                    dve.wait_ge(sem("au_ready"), a.i + 1)
                    v.tensor_scalar(mu[:], bank[1][:, 0:P], bgk[:], 0.0, ALU.add, ALU.min).then_inc(sem("mu_ready"), 1)
                    v.tensor_copy(scores[:, bass.ds(a.i, 1), :].rearrange("p o e -> p (o e)"), bank[1][:, 3 * P:3 * P + E]).then_inc(sem("sc_ready"), 1)
                if B:
                    n = sem("st_steps")
                    wait(dve, sem("o_done"), b.i)
                    wait(dve, n, 5 * b.i)
                    v.scalar_tensor_tensor(sbd[:, 0], rep(tst[:], 1, NH), fac[:], rep(hmask[:], 2, dv), ALU.mult, ALU.mult).then_inc(n, 1)
                    dve.wait_ge(sem("m_done"), b.i + 1)
                    dve.wait_ge(n, 5 * b.i + 1)
                    v.scalar_tensor_tensor(tst[:], tst[:], fac[:], bank[4][:, 0:dv], ALU.mult, ALU.add).then_inc(n, 1)
                    dve.wait_ge(n, 5 * b.i + 2)
                    v.scalar_tensor_tensor(sbd[:, 1], rep(tst[:], 1, NH), eb[:, bp, CH - 1:CH], rep(hmask[:], 2, dv), ALU.mult, ALU.mult).then_inc(n, 1)
                    dve.wait_ge(n, 5 * b.i + 3)
                    v.scalar_tensor_tensor(tst[:], tst[:], eb[:, bp, CH - 1:CH], bank[4][:, dv:2 * dv], ALU.mult, ALU.add).then_inc(n, 1)
                    v.tensor_tensor(fac[:], eb[:, bp, P - 1:P], keep[:, bass.ds(b.i + 1, 1)], ALU.mult).then_inc(n, 1)
                if A:
                    dve.wait_ge(sem("le_ready"), a.i + 1)
                    dve.wait_ge(sem("mu_ready"), a.i + 1)
                    v.tensor_tensor(gl[:], mu[:], le[:], ALU.subtract).then_inc(sem("gl_ready"), 1)
                    dve.wait_ge(sem("gl_ready"), a.i + 1)
                    wait(dve, sem("enb_ready"), a.i)
                    v.tensor_tensor_scan(bs[:], smask[:], gl[:], 0.0, ALU.mult, ALU.add).then_inc(sem("bs_ready"), 1)
                if C:
                    dve.wait_ge(sem("wo_done"), c.i + 1)
                    wait(dve, sem("n_ready"), c.i - 1)
                    wait(dve, sem("base_ready"), c.i - 1)
                    v.tensor_tensor(x2[:, cp, :], bank[7][:, 0:D], xn[:, c.q, :], ALU.add).then_inc(sem("x2_ready"), 1)
                if A:
                    dve.wait_ge(sem("eg_ready"), a.i + 1)
                    v.tensor_scalar(gs1[:], eg[:], 1.0, None, ALU.add).then_inc(sem("gs1_ready"), 1)
                    dve.wait_ge(sem("gs1_ready"), a.i + 1)
                    v.reciprocal(sig[:], gs1[:]).then_inc(sem("sig_ready"), 1)
                    dve.wait_ge(sem("sig_ready"), a.i + 1)
                    wait(dve, sem("og_ready"), a.i - 1)
                    v.tensor_tensor(gs[:, ap, :], bank[2][:, DV:2 * DV], sig[:], ALU.mult).then_inc(sem("gs_ready"), 1)
                    dve.wait_ge(sem("eb_ready"), a.i + 1)
                    wait(dve, sem("qbd_ready"), a.i - 1)
                    wait(dve, sem("o_done"), a.i - 1)
                    v.scalar_tensor_tensor(qe[:, ap, :], bank[1][:, P:2 * P], QSCALE, eb[:, ap, :], ALU.mult, ALU.mult).then_inc(sem("qe_ready"), 1)
                    dve.wait_ge(sem("enb_ready"), a.i + 1)
                    wait(dve, sem("kt_done"), a.i - 1)
                    v.tensor_tensor(ke[:, ap, :], bank[1][:, 2 * P:3 * P], enb[:], ALU.mult).then_inc(sem("ke_ready"), 1)
                if C:
                    dve.wait_ge(sem("s2_ready"), c.i + 1)
                    wait(dve, sem("r2_ready"), c.i - 1)
                    v.tensor_scalar(s2e[:, cp:cp + 1], s2[:, cp:cp + 1], 1.0 / D, 1e-6, ALU.mult, ALU.add).then_inc(sem("s2e_ready"), 1)
                if B:
                    dve.wait_ge(sem("sq_ready"), b.i + 1)
                    v.tensor_reduce(ss[:], sq[:].rearrange("p (h e) -> p h e", h=NH), AX, ALU.add).then_inc(sem("ss_ready"), 1)
                    dve.wait_ge(sem("ss_ready"), b.i + 1)
                    wait(dve, sem("rhp_ready"), b.i)
                    v.tensor_scalar(rh[:], ss[:], 1.0 / dv, 1e-6, ALU.mult, ALU.add).then_inc(sem("rh_ready"), 1)
                if i < NT:
                    dve.wait_ge(sem("sd_ready"), l.i + 1)
                    wait(dve, sem("x2_ready"), l.i - U + 1)
                    wait(dve, sem("xs_ready"), l.i - U + 1)
                    v.tensor_scalar(xn[:, q, :], xin[:, q, :], mv[:, q % 2, 0:1], sd[:, q % 2, 0:1], ALU.subtract, ALU.mult).then_inc(sem("xn_ready"), 1)
                    wait(dve, sem("t1_done"), l.i - 1)
                    wait(dve, sem(f"row_out{q % 2}"), 8 * (l.i - q % 2))
                    v.tensor_scalar(xr[:, q % 2, :], xin[:, q, :], mv[:, q % 2, 0:1], sd[:, q % 2, 1:2], ALU.subtract, ALU.mult).then_inc(sem("xr_ready"), 1)
                if B:
                    dve.wait_ge(sem("rhp_ready"), b.i + 1)
                    wait(dve, sem("og_ready"), b.i)
                    v.tensor_tensor(og1[:].rearrange("p (h e) -> p h e", h=NH), bank[5][:, 0:DV].rearrange("p (h e) -> p h e", h=NH),
                                    rep(rhp[:], 2, dv), ALU.mult).then_inc(sem("og1_ready"), 1)

            for i in range(U):
                body(0, i, i)
                if i == 0:
                    amax_up(0, 0)
                    amax_dn(0)
                if i == 1:
                    scale_up(0, mnw_sb)
                    scale_dn(0)
                if i == 2:
                    lo_up(0, 0)
                    lo_up(0, 1)
                if i == 3:
                    lo_dn(0)
            with dve.Fori(1, NT // U) as h:
                for q in range(U):
                    body(h, q, U + q)
            for i in range(NT, NT + 3):
                body(i // U, i % U, i)

            rs = [0]

            def link(ins):
                rs[0] += 1
                ins.then_inc(sem("rt_steps"), 1)
                dve.wait_ge(sem("rt_steps"), rs[0])

            flat = lambda t: t[:].rearrange("p t e -> p (t e)")
            dve.wait_ge(sem("sc_ready"), NT)

            def pick(src, m, oh):
                link(v.tensor_reduce(m[:], src[:], AX, ALU.max))
                link(v.tensor_tensor(eqm[:], src[:], rep(m[:], 2, E), ALU.is_equal))
                link(v.scalar_tensor_tensor(key[:], eqm[:], float(-E), rep(iota_e8[:], 1, NT), ALU.mult, ALU.add))
                link(v.tensor_reduce(ix[:], key[:], AX, ALU.min))
                link(v.tensor_tensor(oh[:], rep(ix[:], 2, E), rep(iota_e[:], 1, NT), ALU.is_equal))

            pick(scores, m1, oh1)
            link(v.scalar_tensor_tensor(sc2[:], oh1[:], -3.0e38, scores[:], ALU.mult, ALU.add))
            pick(sc2, m2, oh2)
            link(v.tensor_tensor(ohs[:], oh1[:], oh2[:], ALU.add))
            v.tensor_tensor(sc2[:], scores[:], rep(m1[:], 2, E), ALU.subtract).then_inc(sem("rt_ex"), 1)
            v.tensor_tensor(m2[:], m2[:], m1[:], ALU.subtract).then_inc(sem("rt_em2"), 1)
            dve.wait_ge(sem("px_done"), 1)
            link(v.tensor_copy(tot[:], bank[4][:, 256:512].rearrange("p (t e) -> p e t", e=E)))
            link(v.tensor_tensor_scan(inc[:].rearrange("p e t -> p (e t)"), zm[:].rearrange("p e t -> p (e t)"),
                                      tot[:].rearrange("p e t -> p (e t)"), 0.0, ALU.mult, ALU.add))
            link(v.tensor_scalar(pad[:], inc[:, :, NT - 1], float(P - 1), None, ALU.add))
            link(v.tensor_copy(rem[:], pad[:]))
            link(v.tensor_scalar(rem[:], rem[:], 7, 7, ALU.logical_shift_right, ALU.logical_shift_left))
            link(v.tensor_copy(pad[:], rem[:]))
            link(v.tensor_tensor_scan(end[:], ones[:, 0:E], pad[:], 0.0, ALU.mult, ALU.add))
            link(v.tensor_tensor(start[:], end[:], pad[:], ALU.subtract))
            link(v.tensor_tensor(inc[:], inc[:], tot[:], ALU.subtract))
            link(v.tensor_tensor(inc[:], inc[:], rep(start[:], 2, NT), ALU.add))
            link(v.tensor_tensor(key[:], bank[4][:, 0:256].rearrange("p (t e) -> p t e", e=E), inc[:].rearrange("p e t -> p t e"), ALU.add))
            for k, o in enumerate((oh1, oh2)):
                link(v.tensor_tensor(eqm[:], key[:], o[:], ALU.mult))
                link(v.tensor_reduce(slf[:, :, k], eqm[:], AX, ALU.add))
            v.tensor_copy(slot_i[:], slf[:]).then_inc(sem("slots_ready"), 1)
            dve.wait_ge(sem("ex_ready"), 2)
            link(v.tensor_reduce(den[:], ex[:], AX, ALU.add))
            link(v.reciprocal(rden[:], den[:]))
            v.tensor_copy(pairs[:, :, 0, 1].bitcast(F32), rden[:]).then_inc(sem("pair_ready"), 1)
            dve.wait_ge(sem("pair_ready"), 1)
            v.tensor_tensor(pairs[:, :, 1, 1].bitcast(F32), em2[:], rden[:], ALU.mult).then_inc(sem("slots_ready"), 1)
            link(v.tensor_tensor(cmp[:], rep(iota_j[:], 2, E), rep(end[:], 1, MT), ALU.is_ge))
            link(v.tensor_reduce(rj[:], cmp[:], AX, ALU.add))
            link(v.tensor_scalar(rj[:], rj[:], float(E - 1), 1.0, ALU.min, ALU.add))
            v.tensor_copy(etab[:, NT:TT], rj[:]).then_inc(sem("etab_ready"), 1)
            link(v.tensor_tensor(oneh[:], rep(rj[:], 2, E), rep(iota_r[:], 1, MT), ALU.is_equal))
            dve.wait_ge(sem("kap_ready"), 1)
            dve.wait_ge(sem("sd_steps"), 4)
            for n in range(3):
                v.tensor_scalar(tab[:, 0:NT, n], ones[:, 0:NT], ext[:, n, 0:1], None, ALU.mult).then_inc(sem("tab_dense"), 1)
            link(v.tensor_copy(ids2[:, 0:NT], ids[:, 0:NT, 1]))
            amax_up(1, 1)
            phase1_done(dve)

            def step(h, q, i, e=None, more=True):
                t = Tile(h, q)
                u, d, y = t.back(1), t.back(2), t.back(3)
                if i == NT:
                    dve.wait_ge(sem("meta_in"), 16)
                    dve.wait_ge(sem("up_lo"), 2 * R)
                    dve.wait_ge(sem("kap_ready"), R)
                    dve.wait_ge(sem("sd_steps"), 4 * R)
                    prod = stage_u[:, 0, 0:MT * E].rearrange("p (j e) -> p j e", e=E)
                    for n in range(3):
                        link(v.tensor_tensor(prod, oneh[:], rep(ext[:, n, 1:R], 1, MT), ALU.mult))
                        if n < 2:
                            v.tensor_reduce(tab[:, NT:TT, n], prod, AX, ALU.add).then_inc(sem("tab_full"), 1)
                            dve.wait_ge(sem("tab_full"), n + 1)
                        else:
                            link(v.tensor_reduce(ysc[:], prod, AX, ALU.add))
                            v.tensor_tensor(tab[:, NT:TT, 2], ysc[:], meta_sb[:, :, 1].bitcast(F32), ALU.mult).then_inc(sem("tab_full"), 1)
                    v.tensor_copy(ids[:, NT:TT, 0], meta_sb[:, :, 0]).then_inc(sem("tab_full"), 1)
                    link(v.tensor_copy(ids2[:, NT:TT], meta_sb[:, :, 0]))
                if 0 <= i - 2 < TT:
                    for n, (c0, c1, rr_, b_) in enumerate(((0, 4, P, 5), (4, 5, P, 6), (5, 6, HT, 6))):
                        dve.wait_ge(sem("hth_ready"), 3 * d.i + 3)
                        f = 0 if b_ == 5 else (c0 - 4) * P
                        v.tensor_tensor(hT_l[0:rr_, c0:c1, :].rearrange("p c n -> p (c n)"), bank[b_][0:rr_, f:f + (c1 - c0) * P],
                                        hT_h[0:rr_, c0:c1, :].rearrange("p c n -> p (c n)"), ALU.subtract).then_inc(sem("htl_ready"), 1)
                if 0 <= i - 3 < TT:
                    dve.wait_ge(sem("dn_done"), y.i + 1)
                    wait(dve, sem("added"), 16 * y.i)
                    v.tensor_scalar(yo[:, y.q, :], bank[7][:, 0:D], tabslot[:, y.q, 2:3], None, ALU.mult).then_inc(sem("y_ready"), 1)
                if i < TT:
                    dve.wait_ge(sem("xth_ready"), t.i + 1)
                    v.scalar_tensor_tensor(xT_l[:, q % 2].rearrange("p k n -> p (k n)"), bank[0][:, 0:D], XS,
                                           xT_h[:, q % 2].rearrange("p k n -> p (k n)"), ALU.mult, ALU.subtract).then_inc(sem("xtl_ready"), 1)
                if e is not None:
                    if q == 0:
                        scale_up(e, fnw_sb)
                    if q == 1:
                        scale_dn(e)
                        lo_up(e, 0)
                    if q == 2:
                        lo_up(e, 1)
                    if q == 3:
                        lo_dn(e)
                if 0 <= i - 1 < TT:
                    for n, (o, w) in enumerate(SL):
                        dve.wait_ge(sem("sg_ready"), 3 * u.i + n + 1)
                        wait(dve, sem("ht_done"), u.i)
                        v.scalar_tensor_tensor(hid[:, o:o + w], bank[1 + n][:, w:2 * w], tabslot[:, u.q, 1:2], sg[:, o:o + w],
                                               ALU.mult, ALU.mult).then_inc(sem("h_ready"), 1)
                if e is not None:
                    if q == 0:
                        amax_dn(e)
                    if q == 3 and more:
                        amax_up(e + 1, 1)

            run2(dve, step)

        @block.tensor
        def _(pe):
            m = nc.tensor

            def three(outp, hi, lo, whi, wlo, first, last):
                m.matmul(outp, hi, whi, start=first, stop=False, skip_group_check=True)
                m.matmul(outp, hi, wlo, start=False, stop=False, skip_group_check=True)
                return m.matmul(outp, lo, whi, start=False, stop=last, skip_group_check=True)

            pe.wait_ge(wsem, 16 * 12)
            for k in range(KD):
                m.matmul(bank[0][:, k * DK:(k + 1) * DK], gk1_sb[:, k * P:(k + 1) * P], gk2_sb[:], start=True, stop=True).then_inc(sem("gk_done"), 1)
            pe.wait_ge(sem("cst"), NCST)
            pe.wait_ge(sem("w1_lo"), KD)

            def body(h, q, i):
                l = Tile(h, q)
                a, b, c = l.back(1), l.back(2), l.back(3)
                A, B, C = 0 <= i - 1 < NT, 0 <= i - 2 < NT, 0 <= i - 3 < NT
                ap, bp, cp = a.q % 2, b.q % 2, c.q % 2
                if A:
                    pe.wait_ge(sem("xr_ready"), a.i + 1)
                    wait(pe, sem("xl_ready"), a.i)
                    for k in range(KD):
                        ins = m.transpose(bank[0][:, k * P:(k + 1) * P], xr[:, ap, k * P:(k + 1) * P], ident[:])
                    ins.then_inc(sem("t1_done"), 1)
                if B:
                    pe.wait_ge(sem("qbd_ready"), b.i + 1)
                    pe.wait_ge(sem("ke_ready"), b.i + 1)
                    wait(pe, sem("at_ready"), b.i)
                    m.matmul(bank[3][:], ke[:, bp, :], qbd[:, bp].rearrange("p h n -> p (h n)"), start=True, stop=True).then_inc(sem("a_done"), 1)
                    wait(pe, sem("st_steps"), 5 * b.i)
                    m.transpose(bank[4][:, P:2 * P], ke[:, bp, :], ident[:]).then_inc(sem("kt_done"), 1)
                if C:
                    pe.wait_ge(sem("og_ready"), c.i + 1)
                    wait(pe, sem("ol_ready"), c.i)
                    for k in range(KD):
                        ins = m.transpose(bank[6][:, k * P:(k + 1) * P], og[:, cp, k * P:(k + 1) * P], ident[:])
                    ins.then_inc(sem("t2_done"), 1)
                if A:
                    pe.wait_ge(sem("xl_ready"), a.i + 1)
                    wait(pe, sem("ke_ready"), a.i)
                    wait(pe, sem("sc_ready"), a.i)
                    for f in range(3):
                        for k in range(KD):
                            w = slice(f * P, (f + 1) * P)
                            three(bank[1][:, w], w1h[:, k, w], w1l[:, k, w], xh[:, ap, k, :], xl[:, ap, k, :], k == 0, k == KD - 1)
                    for k in range(KD):
                        ins = three(bank[1][:, 3 * P:3 * P + E], xh[:, ap, k, :], xl[:, ap, k, :], w1h[:, k, CR:CO], w1l[:, k, CR:CO], k == 0, k == KD - 1)
                    ins.then_inc(sem("qk_done"), 1)
                    wait(pe, sem("v_ready"), a.i)
                    wait(pe, sem("gs_ready"), a.i)
                    for k in range(KD):
                        ins = three(bank[2][:], xh[:, ap, k, :], xl[:, ap, k, :], w1h[:, k, CV:CR], w1l[:, k, CV:CR], k == 0, k == KD - 1)
                    ins.then_inc(sem("vg_done"), 1)
                if B:
                    pe.wait_ge(sem("ken_ready"), 2 * b.i + 2)
                    pe.wait_ge(sem("v_ready"), b.i + 1)
                    for c_ in range(2):
                        for n in range(NH):
                            ins = m.matmul(bank[4][n * dk:(n + 1) * dk, c_ * dv:(c_ + 1) * dv], ken[:, bp, c_, n * dk:(n + 1) * dk],
                                           v_sb[:, bp, n * dv:(n + 1) * dv], start=True, stop=True)
                    ins.then_inc(sem("m_done"), 1)
                if C:
                    pe.wait_ge(sem("ol_ready"), c.i + 1)
                    wait(pe, sem("x2_ready"), c.i)
                    for k in range(KD):
                        ins = three(bank[7][:, 0:D], oh_[:, k, :], ol_[:, k, :], w1h[:, k, CO:NC1], w1l[:, k, CO:NC1], k == 0, k == KD - 1)
                    ins.then_inc(sem("wo_done"), 1)
                if B:
                    pe.wait_ge(sem("st_steps"), 5 * b.i + 3)
                    pe.wait_ge(sem("at_ready"), b.i + 1)
                    wait(pe, sem("og1_ready"), b.i)
                    for c_ in range(2):
                        m.matmul(bank[5][c_ * CH:(c_ + 1) * CH, 0:DV], qe[:, bp, c_ * CH:(c_ + 1) * CH], sbd[:, c_].rearrange("p h e -> p (h e)"),
                                 start=True, stop=False, skip_group_check=True)
                    for n in range(NH):
                        ins = m.matmul(bank[5][:, n * dv:(n + 1) * dv], at[:, n, :], v_sb[:, bp, n * dv:(n + 1) * dv],
                                       start=False, stop=True, skip_group_check=True)
                    ins.then_inc(sem("o_done"), 1)

            for i in range(U):
                body(0, i, i)
            with pe.Fori(1, NT // U) as h:
                for q in range(U):
                    body(h, q, U + q)
            for i in range(NT, NT + 3):
                body(i // U, i % U, i)
            phase1_done(pe)
            pe.wait_ge(sem("rt_ex"), 1)
            m.matmul(bank[4][:, 0:256], tri[:], ohs[:].rearrange("p t e -> p (t e)"), start=True, stop=True)
            m.matmul(bank[4][:, 256:512], ones[:], ohs[:].rearrange("p t e -> p (t e)"), start=True, stop=True).then_inc(sem("px_done"), 1)
            pe.wait_ge(sem("up_lo"), 2)
            pe.wait_ge(sem("dn_lo"), 1)

            def step(h, q, i, e=None, more=True):
                t = Tile(h, q)
                u, d = t.back(1), t.back(2)
                if 0 <= i - 2 < TT:
                    pe.wait_ge(sem("h_ready"), 3 * d.i + 3)
                    wait(pe, sem("htl_ready"), 3 * d.i)
                    for c in range(KH):
                        w = P if c < KH - 1 else HT
                        ins = m.transpose(bank[5 + c // 4][0:w, (c % 4) * P:(c % 4 + 1) * P], hid[:, c * P:c * P + w], ident[:])
                    ins.then_inc(sem("ht_done"), 1)
                if i < TT:
                    pe.wait_ge(sem(f"x_gat{q}"), 16 * h + 16)
                    wait(pe, sem("xtl_ready"), t.i)
                    for k in range(KD):
                        ins = m.transpose(bank[0][:, k * P:(k + 1) * P], xg[:, q, k * P:(k + 1) * P], ident[:])
                    ins.then_inc(sem("xt_done"), 1)
                if i == NT + 1:
                    pe.wait_ge(sem("up_lo"), 2 * R)
                    pe.wait_ge(sem("dn_lo"), R)
                    pe.wait_ge(sem("etab_ready"), 1)
                if 0 <= i - 1 < TT:
                    r = pe.value_load(etab[0:1, bass.ds(u.i, 1)], min_val=0, max_val=R - 1)
                    pe.wait_ge(sem("xtl_ready"), u.i + 1)
                    for n, (o, w) in enumerate(SL):
                        wait(pe, sem("h_ready"), 3 * (u.i - 1) + n + 1)
                        for k in range(KD):
                            xhi, xlo = xT_h[:, u.q % 2, k, :], xT_l[:, u.q % 2, k, :]
                            ins = three(bank[1 + n][:, 0:2 * w], xhi, xlo, part(r, UPH + k * NUP + 2 * o, 2 * w), part(r, UPL + k * NUP + 2 * o, 2 * w),
                                        k == 0, k == KD - 1)
                        ins.then_inc(sem("up_done"), 1)
                if 0 <= i - 2 < TT:
                    r = pe.value_load(etab[0:1, bass.ds(d.i, 1)], min_val=0, max_val=R - 1)
                    pe.wait_ge(sem("htl_ready"), 3 * d.i + 3)
                    wait(pe, sem("y_ready"), d.i)
                    for c in range(KH):
                        w = P if c < KH - 1 else HT
                        ins = three(bank[7][:, 0:D], hT_h[0:w, c, :], hT_l[0:w, c, :], part(r, DNH + c * D, D, w), part(r, DNL + c * D, D, w),
                                    c == 0, c == KH - 1)
                    ins.then_inc(sem("dn_done"), 1)

            run2(pe, step)


def kernel(**inputs):
    import numpy as np
    import concourse.bacc as _bacc
    from concourse.bass_utils import run_bass_kernel_spmd as _run

    a = {k[3:]: np.asarray(v) for k, v in inputs.items()}
    x = a["attn_hidden_states"]
    B, T, D = x.shape
    chunks = lambda w: np.ascontiguousarray(w.reshape(D // P, P, w.shape[-1]))
    column = lambda w: np.ascontiguousarray(w.reshape(-1, P).T)
    H = a["attn_W_gate"].shape[1]
    cuts = [(0, 256), (256, 512), (512, H)]
    banks = lambda gate, val: np.concatenate([w[:, lo:hi] for lo, hi in cuts for w in (gate, val)], axis=1)
    up = [banks(a["attn_W_gate"], a["attn_W_up"])] + [banks(w[H:].T, w[:H].T) for w in a["ffn_w_up"]]
    arrays = {
        "x": np.ascontiguousarray(x.reshape(B * T, D)),
        "wqk": chunks(np.concatenate([a["attn_Wq"], a["attn_Wk"]], axis=1)),
        "wvg": chunks(np.concatenate([a["attn_Wv"], a["attn_Wg"]], axis=1)),
        "wgk1t": np.ascontiguousarray(a["attn_Wgk1"].T),
        "wgk2": np.ascontiguousarray(a["attn_Wgk2"]),
        "bgk2": column(a["attn_bgk2"]),
        "gnw": np.ascontiguousarray(a["attn_gnorm_w"].reshape(-1, 1)),
        "anw": column(a["attn_attn_norm_w"]),
        "mnw": column(a["attn_mlp_norm_w"]),
        "fnw": column(a["ffn_norm_scale"]),
        "wr": chunks(np.ascontiguousarray(a["ffn_w_router"].T)),
        "wo": chunks(a["attn_Wo"]),
        "wup": np.stack([w.reshape(D // P, P, 2 * H) for w in up]),
        "wdn": np.stack([a["attn_W_down"]] + [w.T for w in a["ffn_w_down"]]),
    }
    nc = _bacc.Bacc("TRN2", target_bir_lowering=False, num_devices=1)
    args = [nc.dram_tensor(f"in_{k}", v.shape, mybir.dt.from_np(v.dtype), kind="ExternalInput").ap() for k, v in arrays.items()]
    args.append(nc.dram_tensor("out_x", (B * T, D), F32, kind="ExternalOutput").ap())
    program(nc, *args)
    r = _run(nc, [{f"in_{k}": v for k, v in arrays.items()}], core_ids=[0])
    return r.results[0]["out_x"].reshape(B, T, D)
```

```python
from contextlib import ExitStack

import concourse.bass as bass
from concourse import mybir

ALU = mybir.AluOpType
ACT = mybir.ActivationFunctionType
AX = mybir.AxisListType.X
RMAX = bass.bass_isa.ReduceOp.max
F32 = mybir.dt.float32
F32R = mybir.dt.float32r
F16 = mybir.dt.float16
I32 = mybir.dt.int32

P = 128
U = 4
XS = 1024.0
WS = 8192.0
TINY = 1e-12


class Tile:

    def __init__(self, h, q):
        self.h, self.q = h, q
        self.i = h * U + q

    def back(self, k):
        d = (self.q - k) // U
        return Tile(self.h + d if d else self.h, (self.q - k) % U)


def wait(eng, sem, value):
    if isinstance(value, int) and value <= 0:
        return
    eng.wait_ge(sem, value)


def rep(ap, axis, n):
    a = ap.unsqueeze(axis)
    shape = list(a.shape)
    shape[axis] = n
    return a.to_broadcast(shape)


def program(nc, x, wqk, wvg, wgk1t, wgk2, bgk2, gnw, anw, mnw, fnw, wr, wo, wup, wdn, out):
    NTOK, D = x.shape
    NT = NTOK // P
    KD = D // P
    E = wr.shape[2]
    NH, TOPK, CH = 4, 2, 64
    DK, DV = wqk.shape[2] // 2, wvg.shape[2] // 2
    dk, dv = DK // NH, DV // NH
    QSCALE = float(dk) ** -0.5
    GSCALE = 1.0 / 16.0
    BT = 1024 // P
    R = E + 1
    NUP = wup.shape[3]
    HID = NUP // 2
    KH = (HID + P - 1) // P
    HT = HID - (KH - 1) * P
    MT = (NTOK * TOPK + E * (P - 1)) // P
    TT = NT + MT
    NSLOT = MT * P
    SL = [(0, 256), (256, 256), (512, HID - 512)]
    UPH, UPL, DNH, DNL = 0, KD * NUP, 2 * KD * NUP, 2 * KD * NUP + KH * D
    RW = DNL + KH * D
    ROW2 = NTOK + P
    assert KD == 2 and KH == 6 and NT == U * E and P == NH * dk and P == 2 * CH

    rows = nc.dram_tensor("rows", (ROW2 + NTOK, D), F32, kind="Internal").ap()
    meta = nc.dram_tensor("meta", (NSLOT, 2), I32, kind="Internal").ap()

    with ExitStack() as ctx:
        def sb(name, shape, dt=F32):
            return ctx.enter_context(nc.sbuf_tensor(name, shape, dt))

        made = {}

        def sem(name):
            if name not in made:
                made[name] = ctx.enter_context(nc.semaphore(name))
            return made[name]

        bank = [ctx.enter_context(nc.psum_tensor(f"bank{n}", [P, 512], F32)) for n in range(8)]

        ident = sb("ident", [P, P])
        ones = sb("ones", [P, P])
        tri = sb("tri", [P, P])
        fnw_sb = sb("fnw_sb", [P, KD])
        mnw_sb = sb("mnw_sb", [P, KD])
        nabs = sb("nabs", [P, 2, KD])
        nneg = sb("nneg", [P, 2, KD])
        scores = sb("scores", [P, NT, E])
        ids = sb("ids", [P, TT, 2], I32)
        tab = sb("tab", [P, TT, 3])
        etab = sb("etab", [P, TT], I32)
        ext = sb("ext", [P, 3, R])
        pairs = sb("pairs", [P, NT, TOPK, 2], I32)
        slot_i = sb("slot_i", [P, NT, TOPK], I32)
        meta_sb = sb("meta_sb", [P, MT, 2], I32)
        oneh = sb("oneh", [P, MT, E])
        iota_r = sb("iota_r", [P, E])
        ids2 = sb("ids2", [P, TT], I32)
        ptok = sb("ptok", [P, U, TOPK, 2], I32)
        pslot = sb("pslot", [P, U, TOPK], I32)
        stage_u = sb("stage_u", [P, KD, NUP])
        stage_d = sb("stage_d", [P, KH, D])
        xg = sb("xg", [P, U, D])
        idslot = sb("idslot", [P, U, 2], I32)
        tabslot = sb("tabslot", [P, U, 3])
        ysc = sb("ysc", [P, MT])
        xT_h = sb("xT_h", [P, 2, KD, P], F16)
        xT_l = sb("xT_l", [P, 2, KD, P], F16)
        sg = sb("sg", [P, HID])
        hid = sb("hid", [P, HID])
        hT_h = sb("hT_h", [P, KH, P], F16)
        hT_l = sb("hT_l", [P, KH, P], F16)
        yo = sb("yo", [P, U, D])
        pm = sb("pm", [P, KD])
        pmn = sb("pmn", [P, KD])
        pr = sb("pr", [P, 2])
        prc = sb("prc", [P, 2])
        am = sb("am", [P, 2])
        amg = sb("amg", [P, 2])
        ia = sb("ia", [P, 2])
        am2 = sb("am2", [P, 1])
        fu = sb("fu", [P, KD])
        fd = sb("fd", [P, 1])
        wall0 = (nc.sbuf_base + 31) // 32 * 32
        wall = nc.alloc_sbuf_tensor_at("wall", [P, R, RW], F16, offset=wall0)
        assert wall0 + R * RW * 2 <= nc.sbuf_usable_end

        place = [wall0 + RW * 2]

        def over(name, shape, dt=F32):
            n = 4
            for s in shape[1:]:
                n *= s
            t = nc.alloc_sbuf_tensor_at(name, shape, dt, offset=place[0])
            place[0] += (n + 31) // 32 * 32
            assert place[0] <= wall0 + R * RW * 2
            return t

        CQ, CK, CV, CR, CO = DK, 2 * DK, 3 * DK, 3 * DK + 2 * DV, 3 * DK + 2 * DV + E
        NC1 = CO + D
        w1r = over("w1r", [P, KD, NC1])
        w1h = over("w1h", [P, KD, NC1], F32R)
        w1l = over("w1l", [P, KD, NC1], F32R)
        gk1_sb = over("gk1_sb", [16, D])
        gk2_sb = over("gk2_sb", [16, DK])
        bgk = over("bgk", [P, 1])
        anw_sb = over("anw_sb", [P, KD])
        gnw_sb = over("gnw_sb", [P, 1])
        cmask = over("cmask", [P, P])
        hmask = over("hmask", [P, NH])
        smask = over("smask", [P, P])
        keep = over("keep", [P, NT + 1])
        xin = over("xin", [P, U, D])
        xn = over("xn", [P, U, D])
        xs = over("xs", [P, U, D])
        st = over("st", [P, 6])
        mv = over("mv", [P, 2, 2])
        sd = over("sd", [P, 2, 2])
        ve = over("ve", [P, 2])
        half = over("half", [P, NH])
        xr = over("xr", [P, 2, D])
        xh = over("xh", [P, 2, KD, P], F32R)
        xl = over("xl", [P, 2, KD, P], F32R)
        au = over("au", [P, P])
        mu = over("mu", [P, P])
        e1 = over("e1", [P, P])
        le = over("le", [P, P])
        gl = over("gl", [P, P])
        bs = over("bs", [P, P])
        eb = over("eb", [P, 2, P])
        enb = over("enb", [P, P])
        qe = over("qe", [P, 2, P])
        ke = over("ke", [P, 2, P])
        qbd = over("qbd", [P, 2, NH, P])
        v_sb = over("v_sb", [P, 2, DV])
        eg = over("eg", [P, DV])
        gs1 = over("gs1", [P, DV])
        gs = over("gs", [P, 2, DV])
        at = over("at", [P, NH, P])
        ken = over("ken", [P, 2, 2, P])
        tst = over("tst", [P, dv])
        fac = over("fac", [P, 1])
        sbd = over("sbd", [P, 2, NH, dv])
        sq = over("sq", [P, DV])
        ss = over("ss", [P, NH])
        rh = over("rh", [P, NH])
        rhp = over("rhp", [P, NH])
        sig = over("sig", [P, DV])
        s2e = over("s2e", [P, 2])
        og1 = over("og1", [P, DV])
        og = over("og", [P, 2, DV])
        oh_ = over("ogT_h", [P, 2, P], F32R)
        ol_ = over("ogT_l", [P, 2, P], F32R)
        x2 = over("x2", [P, 2, D])
        sq2 = over("sq2", [P, D])
        s2 = over("s2", [P, 2])
        r2 = over("r2", [P, 2])
        n_sb = over("n_sb", [P, 2, D])
        b_sb = over("b_sb", [P, 2, D])
        zrow = over("zrow", [P, D])
        padm = over("padm", [P, MT, 2], I32)
        key = over("key", [P, NT, E])
        eqm = over("eqm", [P, NT, E])
        oh1 = over("oh1", [P, NT, E])
        oh2 = over("oh2", [P, NT, E])
        ohs = over("ohs", [P, NT, E])
        sc2 = over("sc2", [P, NT, E])
        ex = over("ex", [P, NT, E])
        m1 = over("m1", [P, NT])
        m2 = over("m2", [P, NT])
        ix = over("ix", [P, NT])
        den = over("den", [P, NT])
        rden = over("rden", [P, NT])
        em2 = over("em2", [P, NT])
        tot = over("tot", [P, E, NT])
        inc = over("inc", [P, E, NT])
        zm = over("zm", [P, E, NT])
        pad = over("pad", [P, E])
        rem = over("rem", [P, E], I32)
        end = over("end", [P, E])
        start = over("start", [P, E])
        slf = over("slf", [P, NT, TOPK])
        iota_e = over("iota_e", [P, E])
        iota_e8 = over("iota_e8", [P, E])
        iota_j = over("iota_j", [P, MT])
        cmp = over("cmp", [P, MT, E])
        rj = over("rj", [P, MT])
        NCST = 14 + 4 + NH + 8

        def part(r, first, n, p=P):
            return wall[0:p, bass.ds(r, 1), first:first + n].rearrange("p o n -> p (o n)")

        def up_ap(e, lo, k):
            return part(e, (UPH, UPL)[lo] + k * NUP, NUP)

        def dn_ap(e, lo):
            return part(e, (DNH, DNL)[lo], KH * D)

        def run2(eng, step, tail=3):
            for i in range(2 * U):
                step(i // U, i % U, i, i // U + 1)
            with eng.Fori(2, E - 1) as h:
                for q in range(U):
                    step(h, q, 2 * U + q, h + 1)
            for q in range(U):
                step(E - 1, q, (E - 1) * U + q, E, False)
            for i in range(NT, NT + 2 * U):
                step(i // U, i % U, i)
            last = (TT - 1) // U
            with eng.Fori(E + 2, last) as h:
                for q in range(U):
                    step(h, q, (E + 2) * U + q)
            for i in range(last * U, TT + tail):
                step(i // U, i % U, i)

        block = ctx.enter_context(nc.Block())

        wsem = sem("weights_loaded")

        def phase1_done(eng):
            eng.wait_ge(sem("wo_done"), NT)
            eng.wait_ge(sem("n_ready"), NT)
            eng.wait_ge(sem("og1_ready"), NT)
            eng.wait_ge(sem("base_ready"), NT)
            for s in range(2):
                eng.wait_ge(sem(f"row_out{s}"), 16 * NT // 2)
                eng.wait_ge(sem(f"n_out{s}"), 16 * NT // 2)
                eng.wait_ge(sem(f"base_out{s}"), 16 * NT // 2)

        @block.sync
        def _(sp):
            for dst, src in (
                (w1r[:, :, CQ:CV], wqk.rearrange("k p n -> p k n")),
                (w1r[:, :, CV:CR], wvg.rearrange("k p n -> p k n")),
                (w1r[:, :, CR:CO], wr.rearrange("k p n -> p k n")),
                (w1r[:, :, CO:NC1], wo.rearrange("k p n -> p k n")),
                (gk1_sb[:], wgk1t), (gk2_sb[:], wgk2), (bgk[:], bgk2),
                (anw_sb[:], anw), (fnw_sb[:], fnw), (mnw_sb[:], mnw),
                (gnw_sb[0:dv, :], gnw), (gnw_sb[dv:2 * dv, :], gnw),
            ):
                sp.dma_start(dst, src).then_inc(wsem, 16)
            sp.dma_start(stage_u[:], wup[0].rearrange("k p n -> p k n")).then_inc(sem("stage_u_in"), 16)
            sp.dma_start(stage_d[:, 0:KH - 1, :], wdn[0, 0:(KH - 1) * P, :].rearrange("(c p) n -> p c n", p=P)).then_inc(sem("stage_d_in"), 16)
            sp.dma_start(stage_d[0:HT, KH - 1, :], wdn[0, (KH - 1) * P:HID, :]).then_inc(sem("stage_d_in"), 16)
            sp.wait_ge(sem("fill_ready"), 1)
            sp.dma_start(rows[NTOK:NTOK + P, :], zrow[:]).then_inc(sem("fill_out"), 16)

            def load(t):
                wait(sp, sem("xs_ready"), t.i - U + 1)
                wait(sp, sem("xr_ready"), t.i - U + 1)
                sp.dma_start(xin[:, t.q, :], x[bass.ds(t.i * P, P), :]).then_inc(sem(f"x_in{t.q}"), 16)

            def body(h, q, i):
                t = Tile(h, q)
                l = t.back(1)
                if i + 2 < NT:
                    load(t.back(-2))
                if 0 <= i - 1 < NT:
                    sp.wait_ge(sem("xr_ready"), l.i + 1)
                    sp.dma_start(rows[bass.ds(l.i * P, P), :], xr[:, l.q % 2, :]).then_inc(sem(f"row_out{l.q % 2}"), 16)
                d = l.back(4)
                if 0 <= i - 5 < NT:
                    sp.wait_ge(sem("n_ready"), d.i + 1)
                    sp.dma_start(rows[bass.ds(d.i * P + ROW2, P), :], n_sb[:, d.q % 2, :]).then_inc(sem(f"n_out{d.q % 2}"), 16)
                    sp.wait_ge(sem("base_ready"), d.i + 1)
                    sp.dma_start(out[bass.ds(d.i * P, P), :], b_sb[:, d.q % 2, :]).then_inc(sem(f"base_out{d.q % 2}"), 16)

            def weights(e):
                sp.wait_ge(sem("up_lo"), 2 * e)
                sp.dma_start(stage_u[:], wup[bass.ds(e, 1), :, :, :].rearrange("o k p n -> p (o k) n")).then_inc(sem("stage_u_in"), 16)
                sp.wait_ge(sem("dn_lo"), e)
                sp.dma_start(stage_d[:, 0:KH - 1, :], wdn[bass.ds(e, 1), 0:(KH - 1) * P, :].rearrange("o (c p) n -> p (o c) n", p=P)).then_inc(sem("stage_d_in"), 16)
                sp.dma_start(stage_d[0:HT, KH - 1, :], wdn[bass.ds(e, 1), (KH - 1) * P:HID, :].rearrange("o p n -> (o p) n")).then_inc(sem("stage_d_in"), 16)

            load(Tile(0, 0))
            load(Tile(0, 1))
            for i in range(2 * U):
                body(i // U, i % U, i)
            with sp.Fori(2, NT // U - 1) as h:
                for q in range(U):
                    body(h, q, 2 * U + q)
            weights(1)
            for i in range(NT - U, NT + 5):
                body(i // U, i % U, i)

            with sp.Fori(2, R) as e:
                weights(e)
            for q in range(U):
                sp.wait_ge(sem(f"meta_out{q}"), 16 * NT * TOPK // U)
            sp.dma_start(meta_sb[:], meta.rearrange("(j p) c -> p j c", p=P)).then_inc(sem("meta_in"), 16)

        @block.gpsimd
        def _(pool):
            g = nc.gpsimd
            g.memset(ident[:], 0.0).then_inc(sem("cst"), 1)
            g.memset(ones[:], 1.0).then_inc(sem("cst"), 1)
            g.memset(smask[:], 1.0).then_inc(sem("cst"), 1)
            g.memset(hmask[:], 0.0).then_inc(sem("cst"), 1)
            g.memset(keep[:], 1.0).then_inc(sem("cst"), 1)
            g.memset(ken[:], 0.0).then_inc(sem("cst"), 1)
            g.memset(tst[:], 0.0).then_inc(sem("cst"), 1)
            g.memset(fac[:], 0.0).then_inc(sem("cst"), 1)
            g.memset(zm[:], 1.0).then_inc(sem("cst"), 1)
            g.memset(half[:], -0.5).then_inc(sem("cst"), 1)
            g.memset(zrow[:], 0.0).then_inc(sem("fill_ready"), 1)
            g.iota(padm[:, :, 0], pattern=[[0, MT]], base=NTOK, channel_multiplier=1).then_inc(sem("padm"), 1)
            g.memset(padm[:, :, 1], 0).then_inc(sem("padm"), 1)
            pool.wait_ge(sem("padm"), 2)
            pool.wait_ge(sem("fill_ready"), 1)
            pool.wait_ge(sem("cst"), 10)
            g.dma_start(meta.rearrange("(j p) c -> p j c", p=P), padm[:]).then_inc(sem("added"), 16)
            g.memset(stage_d[HT:P, KH - 1, :], 0.0).then_inc(sem("cst"), 1)
            pool.wait_ge(sem("cst"), 11)
            g.affine_select(out=ident[:], in_=ident[:], compare_op=ALU.not_equal, fill=1.0, base=0,
                            pattern=[[-1, P]], channel_multiplier=1).then_inc(sem("cst"), 1)
            g.affine_select(out=tri[:], in_=ones[:], compare_op=ALU.is_gt, fill=0.0, base=0,
                            pattern=[[1, P]], channel_multiplier=-1).then_inc(sem("cst"), 1)
            g.affine_select(out=cmask[:], in_=ones[:], compare_op=ALU.is_ge, fill=0.0, base=0,
                            pattern=[[1, P]], channel_multiplier=-1).then_inc(sem("cst"), 1)
            pool.wait_ge(sem("cst"), 14)
            g.memset(cmask[0:CH, CH:P], 0.0).then_inc(sem("cst"), 1)
            pool.wait_ge(sem("cst"), 15)
            g.memset(smask[:, 0:P:CH], 0.0).then_inc(sem("cst"), 1)
            g.memset(keep[:, 0:NT + 1:BT], 0.0).then_inc(sem("cst"), 1)
            g.memset(zm[:, :, 0:1], 0.0).then_inc(sem("cst"), 1)
            for h in range(NH):
                pool.wait_ge(sem("cst"), 18 + h)
                g.memset(hmask[h * dk:(h + 1) * dk, h:h + 1], 1.0).then_inc(sem("cst"), 1)
            pool.wait_ge(sem("cst"), 18 + NH)
            g.iota(iota_e[:], pattern=[[1, E]], base=0, channel_multiplier=0, allow_small_or_imprecise_dtypes=True).then_inc(sem("cst"), 1)
            g.iota(iota_e8[:], pattern=[[1, E]], base=E, channel_multiplier=0, allow_small_or_imprecise_dtypes=True).then_inc(sem("cst"), 1)
            g.iota(iota_r[:], pattern=[[1, E]], base=1, channel_multiplier=0, allow_small_or_imprecise_dtypes=True).then_inc(sem("cst"), 1)
            g.iota(iota_j[:], pattern=[[P, MT]], base=0, channel_multiplier=0, allow_small_or_imprecise_dtypes=True).then_inc(sem("cst"), 1)
            g.iota(ids[:, 0:NT, 0], pattern=[[P, NT]], base=ROW2, channel_multiplier=1).then_inc(sem("cst"), 1)
            g.iota(ids[:, 0:NT, 1], pattern=[[P, NT]], base=0, channel_multiplier=1).then_inc(sem("cst"), 1)
            g.memset(etab[:, 0:NT], 0).then_inc(sem("cst"), 1)
            g.iota(pairs[:, :, :, 0], pattern=[[P, NT], [0, TOPK]], base=0, channel_multiplier=1).then_inc(sem("cst"), 1)

            def allreduce(col):
                g.partition_all_reduce(am[:, col:col + 1], pr[:, col:col + 1], P, RMAX).then_inc(sem("am_up" if col == 0 else "am_dn"), 1)


            def body(h, q, i):
                t = Tile(h, q)
                S = i < NT
                l = t.back(1)
                a, c, d = l.back(1), l.back(3), l.back(4)
                if 0 <= i - 4 < NT:
                    pool.wait_ge(sem("rh_ready"), c.i + 1)
                    wait(pool, sem("og1_ready"), c.i)
                    g.tensor_tensor(rhp[:], rh[:], half[:], ALU.pow).then_inc(sem("rhp_ready"), 1)
                if 0 <= i - 5 < NT:
                    pool.wait_ge(sem("s2e_ready"), d.i + 1)
                    wait(pool, sem("n_ready"), d.i - 1)
                    g.tensor_tensor(r2[:, d.q % 2:d.q % 2 + 1], s2e[:, d.q % 2:d.q % 2 + 1], half[:, 0:1], ALU.pow).then_inc(sem("r2_ready"), 1)
                if 0 <= i - 4 < NT:
                    pool.wait_ge(sem("og1_ready"), c.i + 1)
                    wait(pool, sem("t2_done"), c.i - 1)
                    g.tensor_tensor(og[:, c.q % 2, :], og1[:], gs[:, c.q % 2, :], ALU.mult).then_inc(sem("og_ready"), 1)
                if 0 <= i - 5 < NT:
                    pool.wait_ge(sem("x2_ready"), d.i + 1)
                    wait(pool, sem(f"base_out{(d.q + 1) % 2}"), 8 * (d.i - 1 - (d.q + 1) % 2) + 16)
                    g.tensor_tensor(b_sb[:, d.q % 2, :], x2[:, d.q % 2, :], xs[:, d.q, :], ALU.add).then_inc(sem("base_ready"), 1)
                if S:
                    pool.wait_ge(sem("ve_ready"), 2 * t.i + 2)
                    wait(pool, sem("xr_ready"), t.i - 1)
                    g.tensor_tensor(sd[:, q % 2, :], ve[:], half[:, 0:2], ALU.pow).then_inc(sem("sd_ready"), 1)
                if 0 <= i - 1 < NT:
                    pool.wait_ge(sem("xn_ready"), l.i + 1)
                    wait(pool, sem("base_ready"), l.i - U + 1)
                    g.tensor_tensor(xs[:, l.q, :], xin[:, l.q, :], xn[:, l.q, :], ALU.add).then_inc(sem("xs_ready"), 1)
                if 0 <= i - 2 < NT:
                    pool.wait_ge(sem("qe_ready"), a.i + 1)
                    wait(pool, sem("a_done"), a.i - 1)
                    g.tensor_tensor(qbd[:, a.q % 2, :, :], rep(qe[:, a.q % 2, :], 1, NH), rep(hmask[:], 2, P), ALU.mult).then_inc(sem("qbd_ready"), 1)

            for i in range(2 * U):
                body(i // U, i % U, i)
                if i == 1:
                    pool.wait_ge(sem("pr_up"), 1)
                    allreduce(0)
                    pool.wait_ge(sem("pr_dn"), 1)
                    allreduce(1)
            with pool.Fori(2, NT // U) as h:
                for q in range(U):
                    body(h, q, 2 * U + q)
            for i in range(NT, NT + 5):
                body(i // U, i % U, i)

            phase1_done(pool)
            pool.wait_ge(sem("fill_out"), 16)
            pool.wait_ge(sem("added"), 16)
            pool.wait_ge(sem("slots_ready"), 2)

            def step(h, q, i, e=None, more=True):
                t = Tile(h, q)
                x_, w = t.back(2), t.back(6)

                def scales():
                    g.tensor_copy(tabslot[:, x_.q, :], tab[:, bass.ds(x_.i, 1), :].rearrange("p o c -> p (o c)")).then_inc(sem("tab_ready"), 1)

                if i == NT + 2:
                    pool.wait_ge(sem("tab_full"), 3)
                add = 0 <= i - 6 < TT
                if add:
                    pool.wait_ge(sem("y_ready"), w.i + 1)
                    wait(pool, sem("added"), w.i * 16 + 16)
                    g.tensor_copy(idslot[:, w.q, 1:2], ids2[:, bass.ds(w.i, 1)]).then_inc(sem("sid_ready"), 1)
                if i == NT:
                    scales()
                    pool.wait_ge(sem("ids_full"), 2)
                if i < TT:
                    wait(pool, sem("xt_done"), t.i - 3)
                    g.tensor_copy(idslot[:, q, 0:1], ids[:, bass.ds(t.i, 1), 0]).then_inc(sem("id_ready"), 1)
                if i < NT:
                    wait(pool, sem(f"meta_out{q}"), h * 16 * TOPK)
                    for k in range(TOPK):
                        g.tensor_copy(ptok[:, q, k, :], pairs[:, bass.ds(t.i, 1), k, :].rearrange("p o c -> p (o c)")).then_inc(sem("pt_ready"), 1)
                        g.tensor_copy(pslot[:, q, k:k + 1], slot_i[:, bass.ds(t.i, 1), k]).then_inc(sem("pt_ready"), 1)
                    pool.wait_ge(sem("pt_ready"), (t.i + 1) * 2 * TOPK)
                if add:
                    pool.wait_ge(sem("sid_ready"), w.i + 1)
                if i < TT:
                    pool.wait_ge(sem("id_ready"), t.i + 1)
                if 0 <= i - 2 < TT and i != NT:
                    scales()
                if i < TT:
                    g.indirect_dma_start(out=xg[:, q, :], out_offset=None, in_=rows,
                                         in_offset=bass.IndirectOffsetOnAxis(ap=idslot[:, q, 0:1], axis=0)).then_inc(sem(f"x_gat{q}"), 16)
                if add:
                    g.indirect_dma_start(out=out, out_offset=bass.IndirectOffsetOnAxis(ap=idslot[:, w.q, 1:2], axis=0),
                                         in_=yo[:, w.q, :], in_offset=None, bounds_check=NTOK - 1, oob_is_err=False,
                                         compute_op=ALU.add).then_inc(sem("added"), 16)
                if i < NT:
                    for k in range(TOPK):
                        g.indirect_dma_start(out=meta, out_offset=bass.IndirectOffsetOnAxis(ap=pslot[:, q, k:k + 1], axis=0),
                                             in_=ptok[:, q, k, :], in_offset=None).then_inc(sem(f"meta_out{q}"), 16)
                if e is not None and q in (1, 2):
                    n = q - 1
                    pool.wait_ge(sem("pr_up" if n == 0 else "pr_dn"), e + 1)
                    wait(pool, sem("pr_copied"), 2 * (e - 1) + n)
                    g.tensor_tensor(prc[:, n:n + 1], pr[:, n:n + 1], ones[:, 0:1], ALU.mult).then_inc(sem("pr_copied"), 1)
                    allreduce(n)

            run2(pool, step, 6)
            pool.wait_ge(sem("added"), 16 * TT + 16)

        @block.scalar
        def _(act):
            s = nc.scalar
            act.preload_act_table_set("natural_log_exp_and_others")
            for k in range(KD):
                act.wait_ge(sem("w1_scaled"), k + 1)
                s.activation(w1h[:, k, :], w1r[:, k, :], ACT.Copy).then_inc(sem("w1_hi"), 1)

            def hi_up(e, k):
                act.wait_ge(sem("fu_ready"), e + 1)
                s.activation(up_ap(e, 0, k), stage_u[:, k, :], ACT.Copy, scale=fu[:, k:k + 1]).then_inc(sem("up_hi"), 1)

            def hi_dn(e):
                act.wait_ge(sem("fd_ready"), e + 1)
                s.activation(dn_ap(e, 0), stage_d[:].rearrange("p c n -> p (c n)"), ACT.Copy, scale=fd[:]).then_inc(sem("dn_hi"), 1)

            def body(h, q, i):
                t = Tile(h, q)
                l = t.back(1)
                a, b, c, d = l.back(1), l.back(2), l.back(3), l.back(4)
                A, B, C = 0 <= i - 2 < NT, 0 <= i - 3 < NT, 0 <= i - 4 < NT
                lp, ap, bp, cp, dp = l.q % 2, a.q % 2, b.q % 2, c.q % 2, d.q % 2
                if B:
                    act.wait_ge(sem("kt_done"), b.i + 1)
                    wait(act, sem("m_done"), b.i - 1)
                    s.activation(ken[0:CH, bp, 0, :], bank[4][0:CH, P:2 * P], ACT.Copy).then_inc(sem("ken_ready"), 1)
                    s.activation(ken[CH:P, bp, 1, :], bank[4][CH:P, P:2 * P], ACT.Copy).then_inc(sem("ken_ready"), 1)
                if 0 <= i - 5 < NT:
                    act.wait_ge(sem("x2_ready"), d.i + 1)
                    s.activation(sq2[:], x2[:, dp, :], ACT.Square, accum_out=s2[:, dp:dp + 1]).then_inc(sem("s2_ready"), 1)
                if A:
                    act.wait_ge(sem("qk_done"), a.i + 1)
                    s.activation(au[:], bank[1][:, 0:P], ACT.Abs, bias=bgk[:]).then_inc(sem("au_ready"), 1)
                    act.wait_ge(sem("au_ready"), a.i + 1)
                    s.activation(e1[:], au[:], ACT.Exp, scale=-1.0).then_inc(sem("e1_ready"), 1)
                    act.wait_ge(sem("e1_ready"), a.i + 1)
                    wait(act, sem("gl_ready"), a.i)
                    s.activation(le[:], e1[:], ACT.Ln, bias=ones[:, 0:1]).then_inc(sem("le_ready"), 1)
                if 0 <= i - 1 < NT:
                    act.wait_ge(sem("t1_done"), l.i + 1)
                    wait(act, sem("vg_done"), l.i - 1)
                    s.activation(xh[:, lp].rearrange("p k n -> p (k n)"), bank[0][:, 0:D], ACT.Copy).then_inc(sem("xh_ready"), 1)
                if A:
                    act.wait_ge(sem("vg_done"), a.i + 1)
                    wait(act, sem("m_done"), a.i - 1)
                    wait(act, sem("o_done"), a.i - 1)
                    s.activation(v_sb[:, ap, :], bank[2][:, 0:DV], ACT.Copy).then_inc(sem("v_ready"), 1)
                if C:
                    act.wait_ge(sem("t2_done"), c.i + 1)
                    wait(act, sem("wo_done"), c.i)
                    s.activation(oh_[:].rearrange("p k n -> p (k n)"), bank[6][:, 0:D], ACT.Copy).then_inc(sem("oh_ready"), 1)
                if A:
                    wait(act, sem("lg_ready"), a.i)
                    s.activation(eg[:], bank[2][:, DV:2 * DV], ACT.Exp, scale=-1.0).then_inc(sem("eg_ready"), 1)
                    act.wait_ge(sem("eg_ready"), a.i + 1)
                    wait(act, sem("sig_ready"), a.i)
                    s.activation(gs1[:], eg[:], ACT.Ln, bias=ones[:, 0:1]).then_inc(sem("lg_ready"), 1)
                if A:
                    act.wait_ge(sem("bs_ready"), a.i + 1)
                    wait(act, sem("st_steps"), 5 * (a.i - 1))
                    s.activation(eb[:, ap, :], bs[:], ACT.Exp, scale=GSCALE).then_inc(sem("eb_ready"), 1)
                    wait(act, sem("ke_ready"), a.i)
                    s.activation(enb[:], bs[:], ACT.Exp, scale=-GSCALE).then_inc(sem("enb_ready"), 1)
                if B:
                    act.wait_ge(sem("o_done"), b.i + 1)
                    wait(act, sem("ss_ready"), b.i)
                    s.activation(sq[:], bank[5][:, 0:DV], ACT.Square).then_inc(sem("sq_ready"), 1)
                if 0 <= i - 5 < NT:
                    act.wait_ge(sem("r2_ready"), d.i + 1)
                    wait(act, sem(f"n_out{1 - dp}"), 8 * (d.i - 1 - (1 - dp)) + 16)
                    s.activation(n_sb[:, dp, :], x2[:, dp, :], ACT.Copy, scale=r2[:, dp:dp + 1]).then_inc(sem("n_ready"), 1)
                if A:
                    act.wait_ge(sem("lg_ready"), a.i + 1)
                    wait(act, sem("gs_ready"), a.i)
                    s.activation(sig[:], gs1[:], ACT.Exp, scale=-1.0).then_inc(sem("sig_ready"), 1)

            for i in range(2 * U):
                body(i // U, i % U, i)
                if i == 1:
                    hi_up(0, 0)
                    hi_up(0, 1)
                if i == 2:
                    hi_dn(0)
            with act.Fori(2, NT // U) as h:
                for q in range(U):
                    body(h, q, 2 * U + q)
            for i in range(NT, NT + 5):
                body(i // U, i % U, i)
            act.wait_ge(sem("rt_ex"), 1)
            s.activation(ex[:].rearrange("p t e -> p (t e)"), sc2[:].rearrange("p t e -> p (t e)"), ACT.Exp).then_inc(sem("ex_ready"), 1)
            act.wait_ge(sem("rt_em2"), 1)
            s.activation(em2[:], m2[:], ACT.Exp).then_inc(sem("ex_ready"), 1)
            phase1_done(act)

            def step(h, q, i, e=None, more=True):
                t = Tile(h, q)
                u, d, y = t.back(1), t.back(2), t.back(3)
                if 0 <= i - 2 < TT:
                    act.wait_ge(sem("ht_done"), d.i + 1)
                    wait(act, sem("dn_done"), d.i)
                    s.activation(hT_h[:, 0:4, :].rearrange("p c n -> p (c n)"), bank[5][:], ACT.Copy).then_inc(sem("hth_ready"), 1)
                    s.activation(hT_h[:, 4, :], bank[6][:, 0:P], ACT.Copy).then_inc(sem("hth_ready"), 1)
                    s.activation(hT_h[0:HT, 5, :], bank[6][0:HT, P:2 * P], ACT.Copy).then_inc(sem("hth_ready"), 1)
                if 0 <= i - 3 < TT:
                    act.wait_ge(sem("dn_done"), y.i + 1)
                    wait(act, sem("added"), 16 * (y.i - 2))
                    s.activation(yo[:, y.q, :], bank[7][:, 0:D], ACT.Copy, scale=tabslot[:, y.q, 2:3]).then_inc(sem("y_ready"), 1)
                if i < TT:
                    act.wait_ge(sem("xt_done"), t.i + 1)
                    wait(act, sem("up_done"), 3 * (t.i - 1))
                    s.activation(xT_h[:, q % 2].rearrange("p k n -> p (k n)"), bank[0][:, 0:D], ACT.Copy, scale=XS).then_inc(sem("xth_ready"), 1)
                if 0 <= i - 1 < TT:
                    act.wait_ge(sem("tab_ready"), u.i + 1)
                    for n, (o, w) in enumerate(SL):
                        act.wait_ge(sem("up_done"), 3 * u.i + n + 1)
                        wait(act, sem("h_ready"), 3 * (u.i - 1) + n + 1)
                        s.activation(sg[:, o:o + w], bank[1 + n][:, 0:w], ACT.Silu, scale=tabslot[:, u.q, 0:1]).then_inc(sem("sg_ready"), 1)
                if e is not None:
                    if q == 0:
                        hi_up(e, 0)
                        hi_up(e, 1)
                    if q == 1:
                        hi_dn(e)

            run2(act, step)

        @block.vector
        def _(dve):
            v = nc.vector
            dve.wait_ge(wsem, 16 * 12)
            dve.wait_ge(sem("gk_done"), 2)
            for k in range(KD):
                v.tensor_scalar(w1r[:, k, 0:DK], bank[0][:, k * DK:(k + 1) * DK], anw_sb[:, k:k + 1], None, ALU.mult).then_inc(sem("w1_steps"), 1)
                v.tensor_scalar(w1r[:, k, CQ:CR], w1r[:, k, CQ:CR], anw_sb[:, k:k + 1], None, ALU.mult).then_inc(sem("w1_steps"), 1)
                v.tensor_scalar(w1r[:, k, CR:CO], w1r[:, k, CR:CO], fnw_sb[:, k:k + 1], None, ALU.mult).then_inc(sem("w1_steps"), 1)
                v.tensor_scalar(w1r[:, k, CO:NC1], w1r[:, k, CO:NC1], gnw_sb[:], None, ALU.mult).then_inc(sem("w1_scaled"), 1)
            for n, w in enumerate((mnw_sb, fnw_sb)):
                v.tensor_scalar(nneg[:, n, :], w[:], -1.0, None, ALU.mult).then_inc(sem("nabs_ready"), 1)
                dve.wait_ge(sem("nabs_ready"), 2 * n + 1)
                v.tensor_tensor(nabs[:, n, :], nneg[:, n, :], w[:], ALU.max).then_inc(sem("nabs_ready"), 1)
            dve.wait_ge(sem("w1_steps"), 3 * KD)
            for k in range(KD):
                dve.wait_ge(sem("w1_hi"), k + 1)
                v.tensor_tensor(w1l[:, k, :], w1r[:, k, :], w1h[:, k, :].bitcast(F32), ALU.subtract).then_inc(sem("w1_lo"), 1)
            dve.wait_ge(sem("cst"), NCST)

            def amax_up(e, n):
                dve.wait_ge(sem("stage_u_in"), (e + 1) * 16)
                v.tensor_reduce(pm[:], stage_u[:], AX, ALU.max, apply_absolute_value=True).then_inc(sem("pm_steps"), 1)
                dve.wait_ge(sem("pm_steps"), 2 * e + 1)
                v.tensor_tensor(pmn[:], pm[:], nabs[:, n, :], ALU.mult).then_inc(sem("pm_steps"), 1)
                dve.wait_ge(sem("pm_steps"), 2 * e + 2)
                v.tensor_reduce(pr[:, 0:1], pmn[:], AX, ALU.max).then_inc(sem("pr_up"), 1)

            def amax_dn(e):
                dve.wait_ge(sem("stage_d_in"), (e + 1) * 32)
                v.tensor_reduce(pr[:, 1:2], stage_d[:].rearrange("p c n -> p (c n)"), AX, ALU.max, apply_absolute_value=True).then_inc(sem("pr_dn"), 1)

            def scale_up(e, nw):
                n = sem("su_steps")
                dve.wait_ge(sem("am_up"), e + 1)
                v.tensor_scalar(amg[:, 0:1], am[:, 0:1], TINY, None, ALU.max).then_inc(n, 1)
                dve.wait_ge(n, 3 * e + 1)
                v.reciprocal(ia[:, 0:1], amg[:, 0:1]).then_inc(n, 1)
                v.tensor_scalar(ext[:, 0, bass.ds(e, 1)], amg[:, 0:1], 1.0 / (WS * XS), None, ALU.mult).then_inc(n, 1)
                dve.wait_ge(n, 3 * e + 3)
                v.tensor_scalar(fu[:], nw[:], ia[:, 0:1], WS, ALU.mult, ALU.mult).then_inc(sem("fu_ready"), 1)
                v.tensor_scalar(ext[:, 1, bass.ds(e, 1)], ia[:, 0:1], 0.5 / (WS * XS), None, ALU.mult).then_inc(sem("kap_ready"), 1)

            def scale_dn(e):
                n = sem("sd_steps")
                dve.wait_ge(sem("am_dn"), e + 1)
                v.tensor_scalar(amg[:, 1:2], am[:, 1:2], TINY, None, ALU.max).then_inc(n, 1)
                dve.wait_ge(n, 4 * e + 1)
                v.reciprocal(ia[:, 1:2], amg[:, 1:2]).then_inc(n, 1)
                v.tensor_tensor(am2[:], amg[:, 0:1], amg[:, 0:1], ALU.mult).then_inc(n, 1)
                dve.wait_ge(n, 4 * e + 3)
                v.tensor_scalar(fd[:], ia[:, 1:2], WS, None, ALU.mult).then_inc(sem("fd_ready"), 1)
                v.tensor_scalar(ext[:, 2, bass.ds(e, 1)], am2[:], amg[:, 1:2], 2.0 / WS, ALU.mult, ALU.mult).then_inc(n, 1)

            def lo_up(e, k):
                dve.wait_ge(sem("up_hi"), 2 * e + k + 1)
                v.scalar_tensor_tensor(up_ap(e, 1, k), stage_u[:, k, :], fu[:, k:k + 1], up_ap(e, 0, k), ALU.mult, ALU.subtract).then_inc(sem("up_lo"), 1)

            def lo_dn(e):
                dve.wait_ge(sem("dn_hi"), e + 1)
                v.scalar_tensor_tensor(dn_ap(e, 1), stage_d[:].rearrange("p c n -> p (c n)"), fd[:], dn_ap(e, 0), ALU.mult, ALU.subtract).then_inc(sem("dn_lo"), 1)

            def body(h, q, i):
                t = Tile(h, q)
                S = i < NT
                l = t.back(1)
                a, b, c, d = l.back(1), l.back(2), l.back(3), l.back(4)
                A, B, C = 0 <= i - 2 < NT, 0 <= i - 3 < NT, 0 <= i - 4 < NT
                lp, ap, bp, cp, dp = l.q % 2, a.q % 2, b.q % 2, c.q % 2, d.q % 2
                if C:
                    dve.wait_ge(sem("sq_ready"), c.i + 1)
                    v.tensor_reduce(ss[:], sq[:].rearrange("p (h e) -> p h e", h=NH), AX, ALU.add).then_inc(sem("ss_ready"), 1)
                    dve.wait_ge(sem("ss_ready"), c.i + 1)
                    wait(dve, sem("rhp_ready"), c.i)
                    v.tensor_scalar(rh[:], ss[:], 1.0 / dv, 1e-6, ALU.mult, ALU.add).then_inc(sem("rh_ready"), 1)
                if 0 <= i - 1 < NT:
                    dve.wait_ge(sem("sd_ready"), l.i + 1)
                    wait(dve, sem("t1_done"), l.i - 1)
                    wait(dve, sem(f"row_out{lp}"), 8 * (l.i - lp))
                    v.tensor_scalar(xr[:, lp, :], xin[:, l.q, :], mv[:, lp, 0:1], sd[:, lp, 1:2], ALU.subtract, ALU.mult).then_inc(sem("xr_ready"), 1)
                if 0 <= i - 5 < NT:
                    dve.wait_ge(sem("wo_done"), d.i + 1)
                    wait(dve, sem("n_ready"), d.i - 1)
                    wait(dve, sem("base_ready"), d.i - 1)
                    v.tensor_tensor(x2[:, dp, :], bank[7][:, 0:D], xn[:, d.q, :], ALU.add).then_inc(sem("x2_ready"), 1)
                if 0 <= i - 1 < NT:
                    wait(dve, sem("x2_ready"), l.i - U + 1)
                    wait(dve, sem("xs_ready"), l.i - U + 1)
                    v.tensor_scalar(xn[:, l.q, :], xin[:, l.q, :], mv[:, lp, 0:1], sd[:, lp, 0:1], ALU.subtract, ALU.mult).then_inc(sem("xn_ready"), 1)
                if B:
                    dve.wait_ge(sem("sig_ready"), b.i + 1)
                    wait(dve, sem("og_ready"), b.i - 1)
                    v.tensor_tensor(gs[:, bp, :], bank[2][:, DV:2 * DV], sig[:], ALU.mult).then_inc(sem("gs_ready"), 1)
                if C:
                    dve.wait_ge(sem("rhp_ready"), c.i + 1)
                    wait(dve, sem("og_ready"), c.i)
                    v.tensor_tensor(og1[:].rearrange("p (h e) -> p h e", h=NH), bank[5][:, 0:DV].rearrange("p (h e) -> p h e", h=NH),
                                    rep(rhp[:], 2, dv), ALU.mult).then_inc(sem("og1_ready"), 1)
                if 0 <= i - 5 < NT:
                    dve.wait_ge(sem("s2_ready"), d.i + 1)
                    wait(dve, sem("r2_ready"), d.i - 1)
                    v.tensor_scalar(s2e[:, dp:dp + 1], s2[:, dp:dp + 1], 1.0 / D, 1e-6, ALU.mult, ALU.add).then_inc(sem("s2e_ready"), 1)
                if S:
                    k = sem("ln_steps")
                    dve.wait_ge(sem(f"x_in{q}"), 16 * h + 16)
                    v.bn_stats(st[:], xin[:, q, :]).then_inc(k, 1)
                    dve.wait_ge(k, 2 * t.i + 1)
                if B:
                    n = sem("st_steps")
                    wait(dve, sem("o_done"), b.i)
                    wait(dve, n, 5 * b.i)
                    v.scalar_tensor_tensor(sbd[:, 0], rep(tst[:], 1, NH), fac[:], rep(hmask[:], 2, dv), ALU.mult, ALU.mult).then_inc(n, 1)
                if S:
                    v.bn_aggr(mv[:, q % 2, :], st[:]).then_inc(k, 1)
                if B:
                    dve.wait_ge(sem("a_done"), b.i + 1)
                    wait(dve, sem("o_done"), b.i)
                    v.tensor_tensor(at[:], bank[3][:].rearrange("p (h n) -> p h n", h=NH), rep(cmask[:], 1, NH), ALU.mult).then_inc(sem("at_ready"), 1)
                    dve.wait_ge(sem("m_done"), b.i + 1)
                    dve.wait_ge(n, 5 * b.i + 1)
                    v.scalar_tensor_tensor(tst[:], tst[:], fac[:], bank[4][:, 0:dv], ALU.mult, ALU.add).then_inc(n, 1)
                if B:
                    dve.wait_ge(n, 5 * b.i + 2)
                    v.scalar_tensor_tensor(sbd[:, 1], rep(tst[:], 1, NH), eb[:, bp, CH - 1:CH], rep(hmask[:], 2, dv), ALU.mult, ALU.mult).then_inc(n, 1)
                if S:
                    dve.wait_ge(k, 2 * t.i + 2)
                    wait(dve, sem("sd_ready"), t.i)
                    v.tensor_scalar(ve[:, 0:1], mv[:, q % 2, 1:2], 1e-5, None, ALU.add).then_inc(sem("ve_ready"), 1)
                    v.tensor_scalar(ve[:, 1:2], mv[:, q % 2, 1:2], 1.0 + 1e-6, 1e-11, ALU.mult, ALU.add).then_inc(sem("ve_ready"), 1)
                if A:
                    dve.wait_ge(sem("qk_done"), a.i + 1)
                    dve.wait_ge(sem("au_ready"), a.i + 1)
                    v.tensor_scalar(mu[:], bank[1][:, 0:P], bgk[:], 0.0, ALU.add, ALU.min).then_inc(sem("mu_ready"), 1)
                    v.tensor_copy(scores[:, bass.ds(a.i, 1), :].rearrange("p o e -> p (o e)"), bank[1][:, 3 * P:3 * P + E]).then_inc(sem("sc_ready"), 1)
                if B:
                    dve.wait_ge(n, 5 * b.i + 3)
                    v.scalar_tensor_tensor(tst[:], tst[:], eb[:, bp, CH - 1:CH], bank[4][:, dv:2 * dv], ALU.mult, ALU.add).then_inc(n, 1)
                    v.tensor_tensor(fac[:], eb[:, bp, P - 1:P], keep[:, bass.ds(b.i + 1, 1)], ALU.mult).then_inc(n, 1)
                if A:
                    dve.wait_ge(sem("le_ready"), a.i + 1)
                    dve.wait_ge(sem("mu_ready"), a.i + 1)
                    v.tensor_tensor(gl[:], mu[:], le[:], ALU.subtract).then_inc(sem("gl_ready"), 1)
                    dve.wait_ge(sem("gl_ready"), a.i + 1)
                    wait(dve, sem("enb_ready"), a.i)
                    v.tensor_tensor_scan(bs[:], smask[:], gl[:], 0.0, ALU.mult, ALU.add).then_inc(sem("bs_ready"), 1)
                if C:
                    dve.wait_ge(sem("oh_ready"), c.i + 1)
                    v.tensor_tensor(ol_[:].rearrange("p k n -> p (k n)"), bank[6][:, 0:D],
                                    oh_[:].rearrange("p k n -> p (k n)").bitcast(F32), ALU.subtract).then_inc(sem("ol_ready"), 1)
                if 0 <= i - 1 < NT:
                    dve.wait_ge(sem("xh_ready"), l.i + 1)
                    v.tensor_tensor(xl[:, lp].rearrange("p k n -> p (k n)"), bank[0][:, 0:D],
                                    xh[:, lp].rearrange("p k n -> p (k n)").bitcast(F32), ALU.subtract).then_inc(sem("xl_ready"), 1)
                if A:
                    dve.wait_ge(sem("eb_ready"), a.i + 1)
                    wait(dve, sem("qbd_ready"), a.i - 1)
                    wait(dve, sem("o_done"), a.i - 1)
                    v.scalar_tensor_tensor(qe[:, ap, :], bank[1][:, P:2 * P], QSCALE, eb[:, ap, :], ALU.mult, ALU.mult).then_inc(sem("qe_ready"), 1)
                    dve.wait_ge(sem("enb_ready"), a.i + 1)
                    wait(dve, sem("kt_done"), a.i - 1)
                    v.tensor_tensor(ke[:, ap, :], bank[1][:, 2 * P:3 * P], enb[:], ALU.mult).then_inc(sem("ke_ready"), 1)
            for i in range(2 * U):
                body(i // U, i % U, i)
                if i == 0:
                    amax_up(0, 0)
                    amax_dn(0)
                if i == 1:
                    scale_up(0, mnw_sb)
                    scale_dn(0)
                if i == 2:
                    lo_up(0, 0)
                    lo_up(0, 1)
                if i == 3:
                    lo_dn(0)
            with dve.Fori(2, NT // U) as h:
                for q in range(U):
                    body(h, q, 2 * U + q)
            for i in range(NT, NT + 5):
                body(i // U, i % U, i)

            rs = [0]

            def link(ins):
                rs[0] += 1
                ins.then_inc(sem("rt_steps"), 1)
                dve.wait_ge(sem("rt_steps"), rs[0])

            flat = lambda t: t[:].rearrange("p t e -> p (t e)")
            dve.wait_ge(sem("sc_ready"), NT)

            def pick(src, m, oh):
                link(v.tensor_reduce(m[:], src[:], AX, ALU.max))
                link(v.tensor_tensor(eqm[:], src[:], rep(m[:], 2, E), ALU.is_equal))
                link(v.scalar_tensor_tensor(key[:], eqm[:], float(-E), rep(iota_e8[:], 1, NT), ALU.mult, ALU.add))
                link(v.tensor_reduce(ix[:], key[:], AX, ALU.min))
                link(v.tensor_tensor(oh[:], rep(ix[:], 2, E), rep(iota_e[:], 1, NT), ALU.is_equal))

            pick(scores, m1, oh1)
            link(v.scalar_tensor_tensor(sc2[:], oh1[:], -3.0e38, scores[:], ALU.mult, ALU.add))
            pick(sc2, m2, oh2)
            link(v.tensor_tensor(ohs[:], oh1[:], oh2[:], ALU.add))
            v.tensor_tensor(sc2[:], scores[:], rep(m1[:], 2, E), ALU.subtract).then_inc(sem("rt_ex"), 1)
            v.tensor_tensor(m2[:], m2[:], m1[:], ALU.subtract).then_inc(sem("rt_em2"), 1)
            dve.wait_ge(sem("px_done"), 1)
            link(v.tensor_copy(tot[:], bank[4][:, 256:512].rearrange("p (t e) -> p e t", e=E)))
            link(v.tensor_tensor_scan(inc[:].rearrange("p e t -> p (e t)"), zm[:].rearrange("p e t -> p (e t)"),
                                      tot[:].rearrange("p e t -> p (e t)"), 0.0, ALU.mult, ALU.add))
            link(v.tensor_scalar(pad[:], inc[:, :, NT - 1], float(P - 1), None, ALU.add))
            link(v.tensor_copy(rem[:], pad[:]))
            link(v.tensor_scalar(rem[:], rem[:], 7, 7, ALU.logical_shift_right, ALU.logical_shift_left))
            link(v.tensor_copy(pad[:], rem[:]))
            link(v.tensor_tensor_scan(end[:], ones[:, 0:E], pad[:], 0.0, ALU.mult, ALU.add))
            link(v.tensor_tensor(start[:], end[:], pad[:], ALU.subtract))
            link(v.tensor_tensor(inc[:], inc[:], tot[:], ALU.subtract))
            link(v.tensor_tensor(inc[:], inc[:], rep(start[:], 2, NT), ALU.add))
            link(v.tensor_tensor(key[:], bank[4][:, 0:256].rearrange("p (t e) -> p t e", e=E), inc[:].rearrange("p e t -> p t e"), ALU.add))
            for k, o in enumerate((oh1, oh2)):
                link(v.tensor_tensor(eqm[:], key[:], o[:], ALU.mult))
                link(v.tensor_reduce(slf[:, :, k], eqm[:], AX, ALU.add))
            v.tensor_copy(slot_i[:], slf[:]).then_inc(sem("slots_ready"), 1)
            dve.wait_ge(sem("ex_ready"), 2)
            link(v.tensor_reduce(den[:], ex[:], AX, ALU.add))
            link(v.reciprocal(rden[:], den[:]))
            v.tensor_copy(pairs[:, :, 0, 1].bitcast(F32), rden[:]).then_inc(sem("pair_ready"), 1)
            dve.wait_ge(sem("pair_ready"), 1)
            v.tensor_tensor(pairs[:, :, 1, 1].bitcast(F32), em2[:], rden[:], ALU.mult).then_inc(sem("slots_ready"), 1)
            link(v.tensor_tensor(cmp[:], rep(iota_j[:], 2, E), rep(end[:], 1, MT), ALU.is_ge))
            link(v.tensor_reduce(rj[:], cmp[:], AX, ALU.add))
            link(v.tensor_scalar(rj[:], rj[:], float(E - 1), 1.0, ALU.min, ALU.add))
            v.tensor_copy(etab[:, NT:TT], rj[:]).then_inc(sem("etab_ready"), 1)
            link(v.tensor_tensor(oneh[:], rep(rj[:], 2, E), rep(iota_r[:], 1, MT), ALU.is_equal))
            dve.wait_ge(sem("kap_ready"), 1)
            dve.wait_ge(sem("sd_steps"), 4)
            for n in range(3):
                v.tensor_scalar(tab[:, 0:NT, n], ones[:, 0:NT], ext[:, n, 0:1], None, ALU.mult).then_inc(sem("tab_dense"), 1)
            link(v.tensor_copy(ids2[:, 0:NT], ids[:, 0:NT, 1]))
            amax_up(1, 1)
            phase1_done(dve)

            def step(h, q, i, e=None, more=True):
                t = Tile(h, q)
                u, d, y = t.back(1), t.back(2), t.back(3)
                if 0 <= i - 2 < TT:
                    for n, (c0, c1, rr_, b_) in enumerate(((0, 4, P, 5), (4, 5, P, 6), (5, 6, HT, 6))):
                        dve.wait_ge(sem("hth_ready"), 3 * d.i + 3)
                        f = 0 if b_ == 5 else (c0 - 4) * P
                        v.tensor_tensor(hT_l[0:rr_, c0:c1, :].rearrange("p c n -> p (c n)"), bank[b_][0:rr_, f:f + (c1 - c0) * P],
                                        hT_h[0:rr_, c0:c1, :].rearrange("p c n -> p (c n)"), ALU.subtract).then_inc(sem("htl_ready"), 1)
                if i < TT:
                    dve.wait_ge(sem("xth_ready"), t.i + 1)
                    v.scalar_tensor_tensor(xT_l[:, q % 2].rearrange("p k n -> p (k n)"), bank[0][:, 0:D], XS,
                                           xT_h[:, q % 2].rearrange("p k n -> p (k n)"), ALU.mult, ALU.subtract).then_inc(sem("xtl_ready"), 1)
                if e is not None:
                    if q == 0:
                        scale_up(e, fnw_sb)
                    if q == 1:
                        scale_dn(e)
                        lo_up(e, 0)
                    if q == 2:
                        lo_dn(e)
                if 0 <= i - 1 < TT:
                    for n, (o, w) in enumerate(SL):
                        dve.wait_ge(sem("sg_ready"), 3 * u.i + n + 1)
                        wait(dve, sem("ht_done"), u.i)
                        v.scalar_tensor_tensor(hid[:, o:o + w], bank[1 + n][:, w:2 * w], tabslot[:, u.q, 1:2], sg[:, o:o + w],
                                               ALU.mult, ALU.mult).then_inc(sem("h_ready"), 1)
                if e is not None:
                    if q == 0:
                        amax_dn(e)
                    if q == 1:
                        lo_up(e, 1)
                    if q == 3 and more:
                        amax_up(e + 1, 1)
                if i == NT - 1:
                    dve.wait_ge(sem("meta_in"), 16)
                    v.tensor_copy(ids[:, NT:TT, 0], meta_sb[:, :, 0]).then_inc(sem("ids_full"), 1)
                    v.tensor_copy(ids2[:, NT:TT], meta_sb[:, :, 0]).then_inc(sem("ids_full"), 1)
                    dve.wait_ge(sem("up_lo"), 2 * R)
                    dve.wait_ge(sem("kap_ready"), R)
                    dve.wait_ge(sem("sd_steps"), 4 * R)
                    prod = stage_u[:, 0, 0:MT * E].rearrange("p (j e) -> p j e", e=E)
                    for n in range(3):
                        link(v.tensor_tensor(prod, oneh[:], rep(ext[:, n, 1:R], 1, MT), ALU.mult))
                        if n < 2:
                            v.tensor_reduce(tab[:, NT:TT, n], prod, AX, ALU.add).then_inc(sem("tab_full"), 1)
                            dve.wait_ge(sem("tab_full"), n + 1)
                        else:
                            link(v.tensor_reduce(ysc[:], prod, AX, ALU.add))
                            v.tensor_tensor(tab[:, NT:TT, 2], ysc[:], meta_sb[:, :, 1].bitcast(F32), ALU.mult).then_inc(sem("tab_full"), 1)

            run2(dve, step)

        @block.tensor
        def _(pe):
            m = nc.tensor

            def three(outp, hi, lo, whi, wlo, first, last):
                m.matmul(outp, hi, whi, start=first, stop=False, skip_group_check=True)
                m.matmul(outp, hi, wlo, start=False, stop=False, skip_group_check=True)
                return m.matmul(outp, lo, whi, start=False, stop=last, skip_group_check=True)

            pe.wait_ge(wsem, 16 * 12)
            for k in range(KD):
                m.matmul(bank[0][:, k * DK:(k + 1) * DK], gk1_sb[:, k * P:(k + 1) * P], gk2_sb[:], start=True, stop=True).then_inc(sem("gk_done"), 1)
            pe.wait_ge(sem("cst"), NCST)
            pe.wait_ge(sem("w1_lo"), KD)

            def body(h, q, i):
                t = Tile(h, q)
                l = t.back(1)
                a, b, c = l.back(1), l.back(2), l.back(3)
                A, B, C = 0 <= i - 2 < NT, 0 <= i - 3 < NT, 0 <= i - 4 < NT
                ap, bp, cp = a.q % 2, b.q % 2, c.q % 2
                if B:
                    pe.wait_ge(sem("ke_ready"), b.i + 1)
                    wait(pe, sem("st_steps"), 5 * b.i)
                    m.transpose(bank[4][:, P:2 * P], ke[:, bp, :], ident[:]).then_inc(sem("kt_done"), 1)
                if A:
                    pe.wait_ge(sem("xl_ready"), a.i + 1)
                    wait(pe, sem("ke_ready"), a.i)
                    wait(pe, sem("sc_ready"), a.i)
                    for f in range(3):
                        for k in range(KD):
                            w = slice(f * P, (f + 1) * P)
                            three(bank[1][:, w], w1h[:, k, w], w1l[:, k, w], xh[:, ap, k, :], xl[:, ap, k, :], k == 0, k == KD - 1)
                    for k in range(KD):
                        ins = three(bank[1][:, 3 * P:3 * P + E], xh[:, ap, k, :], xl[:, ap, k, :], w1h[:, k, CR:CO], w1l[:, k, CR:CO], k == 0, k == KD - 1)
                    ins.then_inc(sem("qk_done"), 1)
                if B:
                    pe.wait_ge(sem("qbd_ready"), b.i + 1)
                    wait(pe, sem("at_ready"), b.i)
                    m.matmul(bank[3][:], ke[:, bp, :], qbd[:, bp].rearrange("p h n -> p (h n)"), start=True, stop=True).then_inc(sem("a_done"), 1)
                    pe.wait_ge(sem("ken_ready"), 2 * b.i + 2)
                    pe.wait_ge(sem("v_ready"), b.i + 1)
                    for c_ in range(2):
                        for n in range(NH):
                            ins = m.matmul(bank[4][n * dk:(n + 1) * dk, c_ * dv:(c_ + 1) * dv], ken[:, bp, c_, n * dk:(n + 1) * dk],
                                           v_sb[:, bp, n * dv:(n + 1) * dv], start=True, stop=True)
                    ins.then_inc(sem("m_done"), 1)
                if 0 <= i - 1 < NT:
                    pe.wait_ge(sem("xr_ready"), l.i + 1)
                    wait(pe, sem("xl_ready"), l.i)
                    for k in range(KD):
                        ins = m.transpose(bank[0][:, k * P:(k + 1) * P], xr[:, l.q % 2, k * P:(k + 1) * P], ident[:])
                    ins.then_inc(sem("t1_done"), 1)
                if A:
                    wait(pe, sem("v_ready"), a.i)
                    wait(pe, sem("gs_ready"), a.i)
                    for k in range(KD):
                        ins = three(bank[2][:], xh[:, ap, k, :], xl[:, ap, k, :], w1h[:, k, CV:CR], w1l[:, k, CV:CR], k == 0, k == KD - 1)
                    ins.then_inc(sem("vg_done"), 1)
                if C:
                    pe.wait_ge(sem("og_ready"), c.i + 1)
                    wait(pe, sem("ol_ready"), c.i)
                    for k in range(KD):
                        ins = m.transpose(bank[6][:, k * P:(k + 1) * P], og[:, cp, k * P:(k + 1) * P], ident[:])
                    ins.then_inc(sem("t2_done"), 1)
                if B:
                    pe.wait_ge(sem("st_steps"), 5 * b.i + 3)
                    pe.wait_ge(sem("at_ready"), b.i + 1)
                    wait(pe, sem("og1_ready"), b.i)
                    for c_ in range(2):
                        m.matmul(bank[5][c_ * CH:(c_ + 1) * CH, 0:DV], qe[:, bp, c_ * CH:(c_ + 1) * CH], sbd[:, c_].rearrange("p h e -> p (h e)"),
                                 start=True, stop=False, skip_group_check=True)
                    for n in range(NH):
                        ins = m.matmul(bank[5][:, n * dv:(n + 1) * dv], at[:, n, :], v_sb[:, bp, n * dv:(n + 1) * dv],
                                       start=False, stop=True, skip_group_check=True)
                    ins.then_inc(sem("o_done"), 1)
                if C:
                    pe.wait_ge(sem("ol_ready"), c.i + 1)
                    wait(pe, sem("x2_ready"), c.i)
                    for k in range(KD):
                        ins = three(bank[7][:, 0:D], oh_[:, k, :], ol_[:, k, :], w1h[:, k, CO:NC1], w1l[:, k, CO:NC1], k == 0, k == KD - 1)
                    ins.then_inc(sem("wo_done"), 1)

            for i in range(2 * U):
                body(i // U, i % U, i)
            with pe.Fori(2, NT // U) as h:
                for q in range(U):
                    body(h, q, 2 * U + q)
            for i in range(NT, NT + 5):
                body(i // U, i % U, i)
            phase1_done(pe)
            pe.wait_ge(sem("rt_ex"), 1)
            m.matmul(bank[4][:, 0:256], tri[:], ohs[:].rearrange("p t e -> p (t e)"), start=True, stop=True)
            m.matmul(bank[4][:, 256:512], ones[:], ohs[:].rearrange("p t e -> p (t e)"), start=True, stop=True).then_inc(sem("px_done"), 1)
            pe.wait_ge(sem("up_lo"), 2)
            pe.wait_ge(sem("dn_lo"), 1)

            def step(h, q, i, e=None, more=True):
                t = Tile(h, q)
                u, d = t.back(1), t.back(2)
                if i == NT + 1:
                    pe.wait_ge(sem("up_lo"), 2 * R)
                    pe.wait_ge(sem("dn_lo"), R)
                    pe.wait_ge(sem("etab_ready"), 1)
                if 0 <= i - 1 < TT:
                    ru = pe.value_load(etab[0:1, bass.ds(u.i, 1)], min_val=0, max_val=R - 1)
                if 0 <= i - 2 < TT:
                    rd = pe.value_load(etab[0:1, bass.ds(d.i, 1)], min_val=0, max_val=R - 1)
                if 0 <= i - 2 < TT:
                    pe.wait_ge(sem("h_ready"), 3 * d.i + 3)
                    wait(pe, sem("htl_ready"), 3 * d.i)
                    for c in range(KH):
                        w = P if c < KH - 1 else HT
                        ins = m.transpose(bank[5 + c // 4][0:w, (c % 4) * P:(c % 4 + 1) * P], hid[:, c * P:c * P + w], ident[:])
                    ins.then_inc(sem("ht_done"), 1)
                if i < TT:
                    pe.wait_ge(sem(f"x_gat{q}"), 16 * h + 16)
                    wait(pe, sem("xtl_ready"), t.i)
                    for k in range(KD):
                        ins = m.transpose(bank[0][:, k * P:(k + 1) * P], xg[:, q, k * P:(k + 1) * P], ident[:])
                    ins.then_inc(sem("xt_done"), 1)
                if 0 <= i - 1 < TT:
                    pe.wait_ge(sem("xtl_ready"), u.i + 1)
                    for n, (o, w) in enumerate(SL):
                        wait(pe, sem("h_ready"), 3 * (u.i - 1) + n + 1)
                        for k in range(KD):
                            xhi, xlo = xT_h[:, u.q % 2, k, :], xT_l[:, u.q % 2, k, :]
                            ins = three(bank[1 + n][:, 0:2 * w], xhi, xlo, part(ru, UPH + k * NUP + 2 * o, 2 * w), part(ru, UPL + k * NUP + 2 * o, 2 * w),
                                        k == 0, k == KD - 1)
                        ins.then_inc(sem("up_done"), 1)
                if 0 <= i - 2 < TT:
                    pe.wait_ge(sem("htl_ready"), 3 * d.i + 3)
                    wait(pe, sem("y_ready"), d.i)
                    for c in range(KH):
                        w = P if c < KH - 1 else HT
                        ins = three(bank[7][:, 0:D], hT_h[0:w, c, :], hT_l[0:w, c, :], part(rd, DNH + c * D, D, w), part(rd, DNL + c * D, D, w),
                                    c == 0, c == KH - 1)
                    ins.then_inc(sem("dn_done"), 1)

            run2(pe, step)


def kernel(**inputs):
    import numpy as np
    import concourse.bacc as _bacc
    from concourse.bass_utils import run_bass_kernel_spmd as _run

    a = {k[3:]: np.asarray(v) for k, v in inputs.items()}
    x = a["attn_hidden_states"]
    B, T, D = x.shape
    chunks = lambda w: np.ascontiguousarray(w.reshape(D // P, P, w.shape[-1]))
    column = lambda w: np.ascontiguousarray(w.reshape(-1, P).T)
    H = a["attn_W_gate"].shape[1]
    cuts = [(0, 256), (256, 512), (512, H)]
    banks = lambda gate, val: np.concatenate([w[:, lo:hi] for lo, hi in cuts for w in (gate, val)], axis=1)
    up = [banks(a["attn_W_gate"], a["attn_W_up"])] + [banks(w[H:].T, w[:H].T) for w in a["ffn_w_up"]]
    arrays = {
        "x": np.ascontiguousarray(x.reshape(B * T, D)),
        "wqk": chunks(np.concatenate([a["attn_Wq"], a["attn_Wk"]], axis=1)),
        "wvg": chunks(np.concatenate([a["attn_Wv"], a["attn_Wg"]], axis=1)),
        "wgk1t": np.ascontiguousarray(a["attn_Wgk1"].T),
        "wgk2": np.ascontiguousarray(a["attn_Wgk2"]),
        "bgk2": column(a["attn_bgk2"]),
        "gnw": np.ascontiguousarray(a["attn_gnorm_w"].reshape(-1, 1)),
        "anw": column(a["attn_attn_norm_w"]),
        "mnw": column(a["attn_mlp_norm_w"]),
        "fnw": column(a["ffn_norm_scale"]),
        "wr": chunks(np.ascontiguousarray(a["ffn_w_router"].T)),
        "wo": chunks(a["attn_Wo"]),
        "wup": np.stack([w.reshape(D // P, P, 2 * H) for w in up]),
        "wdn": np.stack([a["attn_W_down"]] + [w.T for w in a["ffn_w_down"]]),
    }
    nc = _bacc.Bacc("TRN2", target_bir_lowering=False, num_devices=1)
    args = [nc.dram_tensor(f"in_{k}", v.shape, mybir.dt.from_np(v.dtype), kind="ExternalInput").ap() for k, v in arrays.items()]
    args.append(nc.dram_tensor("out_x", (B * T, D), F32, kind="ExternalOutput").ap())
    program(nc, *args)
    r = _run(nc, [{f"in_{k}": v for k, v in arrays.items()}], core_ids=[0])
    return r.results[0]["out_x"].reshape(B, T, D)
```
